# Optimizing a Trainium2 kernel written in Bass

```python
import numpy as np
import jax
import jax.numpy as jnp

def _softmax(x, axis=-1):
    return jax.nn.softmax(x, axis=axis)

def _gelu(x):
    return jax.nn.gelu(x, approximate=True)

def _silu(x):
    return jax.nn.silu(x)

def _sigmoid(x):
    return jax.nn.sigmoid(x)

def _layernorm(x, axis=-1, eps=1e-05):
    m = jnp.mean(x, axis=axis, keepdims=True)
    v = jnp.var(x, axis=axis, keepdims=True)
    return (x - m) / jnp.sqrt(v + eps)

def _scatter_add(tgt, idx, src, axis=0):
    return tgt.at[idx].add(src)

def _segment_sum(src, seg, n):
    return jax.ops.segment_sum(src, seg, n)
kernel_name = 'mk_decoder_preln_d1_seqx_r8_ff6b5f'

def setup_inputs(seed: int=0):
    np.random.seed(seed)
    _w = jnp.asarray

    def _rec_inputs():
        import jax
        import jax.numpy as jnp
        _rk = jax.random.key(seed)
        x = -0.0003929 + 0.9999 * jax.random.normal(jax.random.fold_in(_rk, 1), (2, 512, 128), jnp.float32)
        _lenS = 512 - jax.random.randint(jax.random.fold_in(_rk, 7), (2,), 0, max(1, 512 // 4) + 1, jnp.int32)
        _lenS2 = 154 - jax.random.randint(jax.random.fold_in(_rk, 8), (2,), 0, max(1, 154 // 4) + 1, jnp.int32)
        _ctx_768P = jax.random.normal(jax.random.fold_in(_rk, 11), (2, 16, 96), jnp.float32)
        _ctx_768c = jax.random.dirichlet(jax.random.fold_in(_rk, 511), 0.3 * jnp.ones((16,), jnp.float32), (2, 154))
        _ctx_768t = jnp.einsum('bsk,bkd->bsd', _ctx_768c, _ctx_768P)
        _ctx_768t = _ctx_768t * jax.lax.rsqrt(jnp.mean(jnp.square(_ctx_768t)) + 1e-12) * 0.953939
        ctx_768 = -0.00055796 + 0.999787 * (_ctx_768t + 0.3 * jax.random.normal(jax.random.fold_in(_rk, 611), (2, 154, 96), jnp.float32))
        return (x, ctx_768)
    x, ctx_768 = _rec_inputs()

    def _L0_attn_setup():
        import jax, jax.numpy as jnp
        import numpy as np
        HEADS = 16
        PHI = (1.0 + np.sqrt(5.0)) / 2.0

        def phi_bias(L):
            pos = jnp.arange(L, dtype=jnp.float32) * PHI % 1.0
            dist = jnp.abs(pos[:, None] - pos[None, :])
            return jnp.log(jnp.exp(-dist) + 1e-08)
        key = jax.random.key(seed)
        k1, k2, k3, k4 = jax.random.split(key, 4)
        B, L, D = (2, 256, 128)
        x = jax.random.normal(k1, (B, L, D), dtype=jnp.float32)
        w_qkv = jax.random.normal(k2, (D, 3 * D), dtype=jnp.float32) * D ** (-0.5)
        w_proj = jax.random.normal(k3, (D, D), dtype=jnp.float32) * D ** (-0.5)
        b_proj = jax.random.normal(k4, (D,), dtype=jnp.float32) * 0.01
        return {'x': x, 'w_qkv': w_qkv, 'w_proj': w_proj, 'b_proj': b_proj}
    _L0_attn_all = _L0_attn_setup()
    _L0_attn_in = {k: v for k, v in _L0_attn_all.items() if k in ('w_qkv', 'w_proj', 'b_proj')}
    del _L0_attn_all

    def _L0_xattn_setup():
        import jax, jax.numpy as jnp
        import numpy as np
        D = 128
        L = 96
        H = 16
        EPS = 1e-05

        def layer_norm(x, g, b):
            mu = jnp.mean(x, axis=-1, keepdims=True)
            var = jnp.var(x, axis=-1, keepdims=True)
            return (x - mu) * jax.lax.rsqrt(var + EPS) * g + b
        key = jax.random.key(seed)
        ks = jax.random.split(key, 8)
        B, T, N = (4, 512, 64)
        sq = lambda d: 1.0 / np.sqrt(d)
        return {'x': jax.random.normal(ks[0], (B, T, D), jnp.float32), 'xf': jax.random.normal(ks[1], (B, N, L), jnp.float32), 'norm_g': jnp.ones((D,), jnp.float32), 'norm_b': jnp.zeros((D,), jnp.float32), 'tnorm_g': jnp.ones((L,), jnp.float32), 'tnorm_b': jnp.zeros((L,), jnp.float32), 'Wq': jax.random.normal(ks[2], (D, D), jnp.float32) * sq(D), 'bq': jnp.zeros((D,), jnp.float32), 'Wk': jax.random.normal(ks[3], (L, D), jnp.float32) * sq(L), 'bk': jnp.zeros((D,), jnp.float32), 'Wv': jax.random.normal(ks[4], (L, D), jnp.float32) * sq(L), 'bv': jnp.zeros((D,), jnp.float32)}
    _L0_xattn_all = _L0_xattn_setup()
    _L0_xattn_in = {k: v for k, v in _L0_xattn_all.items() if k in ('norm_g', 'norm_b', 'tnorm_g', 'tnorm_b', 'Wq', 'bq', 'Wk', 'bk', 'Wv', 'bv')}
    del _L0_xattn_all

    def _L0_ffn_setup():
        import jax, jax.numpy as jnp
        import numpy as np
        B, T, C, E, K, CAP, H = (8, 256, 128, 8, 2, 512, 512)
        key = jax.random.key(seed)
        ks = jax.random.split(key, 6)
        s = 0.02
        return {'x': jax.random.normal(ks[0], (B, T, C), jnp.float32), 'rw1': s * jax.random.normal(ks[1], (C, H), jnp.float32), 'rb1': jnp.zeros((H,), jnp.float32), 'rw2': s * jax.random.normal(ks[2], (H, E), jnp.float32), 'rb2': jnp.zeros((E,), jnp.float32), 'ew1': s * jax.random.normal(ks[3], (E, C, H), jnp.float32), 'eb1': jnp.zeros((E, H), jnp.float32), 'ew2': s * jax.random.normal(ks[4], (E, H, C), jnp.float32), 'eb2': jnp.zeros((E, C), jnp.float32)}
    _L0_ffn_all = _L0_ffn_setup()
    _L0_ffn_in = {k: v for k, v in _L0_ffn_all.items() if k in ('rw1', 'rb1', 'rw2', 'rb2', 'ew1', 'eb1', 'ew2', 'eb2')}
    del _L0_ffn_all
    return {'x': x, 'ctx_768': ctx_768, 'L0_attn_w_qkv': _L0_attn_in['w_qkv'], 'L0_attn_w_proj': _L0_attn_in['w_proj'], 'L0_attn_b_proj': _L0_attn_in['b_proj'], 'L0_xattn_norm_g': _L0_xattn_in['norm_g'], 'L0_xattn_norm_b': _L0_xattn_in['norm_b'], 'L0_xattn_tnorm_g': _L0_xattn_in['tnorm_g'], 'L0_xattn_tnorm_b': _L0_xattn_in['tnorm_b'], 'L0_xattn_Wq': _L0_xattn_in['Wq'], 'L0_xattn_bq': _L0_xattn_in['bq'], 'L0_xattn_Wk': _L0_xattn_in['Wk'], 'L0_xattn_bk': _L0_xattn_in['bk'], 'L0_xattn_Wv': _L0_xattn_in['Wv'], 'L0_xattn_bv': _L0_xattn_in['bv'], 'L0_ffn_rw1': _L0_ffn_in['rw1'], 'L0_ffn_rb1': _L0_ffn_in['rb1'], 'L0_ffn_rw2': _L0_ffn_in['rw2'], 'L0_ffn_rb2': _L0_ffn_in['rb2'], 'L0_ffn_ew1': _L0_ffn_in['ew1'], 'L0_ffn_eb1': _L0_ffn_in['eb1'], 'L0_ffn_ew2': _L0_ffn_in['ew2'], 'L0_ffn_eb2': _L0_ffn_in['eb2']}

def reference(x, ctx_768, L0_attn_w_qkv, L0_attn_w_proj, L0_attn_b_proj, L0_xattn_norm_g, L0_xattn_norm_b, L0_xattn_tnorm_g, L0_xattn_tnorm_b, L0_xattn_Wq, L0_xattn_bq, L0_xattn_Wk, L0_xattn_bk, L0_xattn_Wv, L0_xattn_bv, L0_ffn_rw1, L0_ffn_rb1, L0_ffn_rw2, L0_ffn_rb2, L0_ffn_ew1, L0_ffn_eb1, L0_ffn_ew2, L0_ffn_eb2):
    import jax
    import jax.numpy as jnp

    def _L0_attn_ref(x, w_qkv, w_proj, b_proj):
        import jax, jax.numpy as jnp
        import numpy as np
        HEADS = 16
        PHI = (1.0 + np.sqrt(5.0)) / 2.0

        def phi_bias(L):
            pos = jnp.arange(L, dtype=jnp.float32) * PHI % 1.0
            dist = jnp.abs(pos[:, None] - pos[None, :])
            return jnp.log(jnp.exp(-dist) + 1e-08)
        B, L, D = x.shape
        H = HEADS
        Dh = D // H
        scale = Dh ** (-0.5)
        qkv = (x @ w_qkv).reshape(B, L, 3, H, Dh)
        q = jnp.transpose(qkv[:, :, 0], (0, 2, 1, 3))
        k = jnp.transpose(qkv[:, :, 1], (0, 2, 1, 3))
        v = jnp.transpose(qkv[:, :, 2], (0, 2, 1, 3))
        attn = jnp.einsum('bhid,bhjd->bhij', q, k) * scale
        attn = attn + phi_bias(L)[None, None]
        attn = jax.nn.softmax(attn, axis=-1)
        out = jnp.einsum('bhij,bhjd->bhid', attn, v)
        out = jnp.transpose(out, (0, 2, 1, 3)).reshape(B, L, D)
        return out @ w_proj + b_proj

    def _L0_xattn_ref(x, xf, norm_g, norm_b, tnorm_g, tnorm_b, Wq, bq, Wk, bk, Wv, bv):
        import jax, jax.numpy as jnp
        import numpy as np
        D = 128
        L = 96
        H = 16
        EPS = 1e-05

        def layer_norm(x, g, b):
            mu = jnp.mean(x, axis=-1, keepdims=True)
            var = jnp.var(x, axis=-1, keepdims=True)
            return (x - mu) * jax.lax.rsqrt(var + EPS) * g + b
        B, T, _ = x.shape
        N = xf.shape[1]
        hd = D // H
        xn = layer_norm(x, norm_g, norm_b)
        xfn = layer_norm(xf, tnorm_g, tnorm_b)
        q = (xn @ Wq + bq).reshape(B, T, H, hd)
        k = (xfn @ Wk + bk).reshape(B, N, H, hd)
        v = (xfn @ Wv + bv).reshape(B, N, H, hd)
        scores = jnp.einsum('bthd,bnhd->bhtn', q, k) / jnp.sqrt(jnp.float32(hd))
        w = jax.nn.softmax(scores, axis=-1)
        y = jnp.einsum('bhtn,bnhd->bthd', w, v).reshape(B, T, D)
        return y

    def _L0_ffn_ref(x, rw1, rb1, rw2, rb2, ew1, eb1, ew2, eb2):
        import jax, jax.numpy as jnp
        import numpy as np
        B, T, C, E, K, CAP, H = (8, 256, 128, 8, 2, 512, 512)
        Bx, Tx, Cx = x.shape
        N = Bx * Tx
        logits = jax.nn.relu(x @ rw1 + rb1) @ rw2 + rb2
        vals, ids = jax.lax.top_k(logits, K)
        probs = jax.nn.softmax(vals, axis=-1)
        ids_f = ids.reshape(N * K)
        probs_f = probs.reshape(N * K)
        xr = jnp.repeat(x.reshape(N, Cx), K, axis=0)
        m = jax.nn.one_hot(ids_f, E, dtype=jnp.int32)
        pos = jnp.cumsum(m, axis=0) - 1
        pos_tok = jnp.take_along_axis(pos, ids_f[:, None], axis=1)[:, 0]
        keep = (pos_tok < CAP).astype(x.dtype)
        pos_c = jnp.clip(pos_tok, 0, CAP - 1)
        disp = jnp.zeros((E, CAP, Cx), x.dtype).at[ids_f, pos_c].add(xr * keep[:, None])
        h = jax.nn.relu(jnp.einsum('enc,ech->enh', disp, ew1) + eb1[:, None, :])
        eo = jnp.einsum('enh,ehc->enc', h, ew2) + eb2[:, None, :]
        y = eo[ids_f, pos_c] * (probs_f * keep)[:, None]
        return y.reshape(Bx, Tx, K, Cx).sum(axis=2)
    x = x + _L0_attn_ref(_layernorm(x, axis=-1), L0_attn_w_qkv, L0_attn_w_proj, L0_attn_b_proj)
    x = x + _L0_xattn_ref(_layernorm(x, axis=-1), ctx_768, L0_xattn_norm_g, L0_xattn_norm_b, L0_xattn_tnorm_g, L0_xattn_tnorm_b, L0_xattn_Wq, L0_xattn_bq, L0_xattn_Wk, L0_xattn_bk, L0_xattn_Wv, L0_xattn_bv)
    x = x + _L0_ffn_ref(_layernorm(x, axis=-1), L0_ffn_rw1, L0_ffn_rb1, L0_ffn_rw2, L0_ffn_rb2, L0_ffn_ew1, L0_ffn_eb1, L0_ffn_ew2, L0_ffn_eb2)
    return x

_drawn_inputs = setup_inputs


def setup_inputs(seed=0):
    import zlib

    import numpy as np

    out = dict(_drawn_inputs(seed))
    spreads = {'L0_xattn_norm_g': (1.0, 0.2),
     'L0_xattn_norm_b': (0.0, 0.522),
     'L0_xattn_tnorm_g': (1.0, 0.2),
     'L0_xattn_tnorm_b': (0.0, 0.1),
     'L0_xattn_bq': (0.0, 0.453),
     'L0_xattn_bk': (0.0, 0.8),
     'L0_xattn_bv': (0.0, 0.1),
     'L0_ffn_rb1': (0.0, 0.1),
     'L0_ffn_rb2': (0.0, 0.1),
     'L0_ffn_eb1': (0.0, 0.523),
     'L0_ffn_eb2': (0.0, 0.1)}
    factors = {'L0_attn_b_proj': 5.573}
    for name, (base, spread) in spreads.items():
        noise = np.random.default_rng([zlib.crc32(name.encode()), seed]).standard_normal(out[name].shape)
        drawn = base * np.exp(spread * noise) if base else spread * noise
        out[name] = jnp.asarray(drawn.astype(out[name].dtype))
    for name, factor in factors.items():
        out[name] = (out[name] * factor).astype(out[name].dtype)
    return out
```

```python
from contextlib import ExitStack

import concourse.bass as bass
import numpy as np
from concourse import mybir

F32 = mybir.dt.float32
F16 = mybir.dt.float16
BF16 = mybir.dt.bfloat16
I32 = mybir.dt.int32
U32 = mybir.dt.uint32
ALU = mybir.AluOpType
ACT = mybir.ActivationFunctionType
AX = mybir.AxisListType

P = 128
B = 2
L = 512
D = 128
H = 16
DH = D // H
TT = L // P
NT = B * TT
HG = 4
G = H // HG
KC = L // P
NC = 154
CD = 96
NCB = NC - P
CW = P + 32
E = 8
F = 512
M = F // P
CAP = 512
EPS = 1e-5
SCALE = float(DH) ** -0.5
NB = 3
NS = 3
NP = 2
LIMIT = 60.0
SHIFT = 64.0
VROWS = 42


def weave(main, filler, per):
    out = []
    for step in main:
        out.append(step)
        for _ in range(per):
            if filler:
                out.append(filler.pop(0))
    return out


def schedule():

    def attention(b):
        units = [(g, c) for g in range(G) for c in range(KC)]
        out = []
        for i, (g, c) in enumerate(units):
            out.append([("scores1", b, g, c)])
            if i > 0:
                out[-1].append(("values1", b, *units[i - 1]))
            if c == 0 and g > 0:
                out[-1].append(("out1", b, g - 1))
            if c == 1 and g > 0:
                out[-1].append(("heads1", b, g - 1))
        return out + [[("values1", b, *units[-1]), ("out1", b, G - 1)], [("heads1", b, G - 1)]]

    def after_attention(b):
        return [("joined", b), ("project", b), ("norm2", b), ("turn2", b), ("query2", b), ("sizes", b + B)] + \
               [("spread2", b, g) for g in range(G)] + [("flag", b + B), ("guard", b + B)]

    def cross(b):
        out = []
        for g in range(G + 1):
            if g < G:
                out.append(("scores2", b, g))
            if g > 0:
                out += [("values2", b, g - 1), ("out2", b, g - 1)]
            if g > 1:
                out.append(("heads2", b, g - 2))
        return out + [("heads2", b, G - 1)]

    def router(b):
        return [("norm3", b), ("turn3", b)] + [("router_hidden", b, m) for m in range(M)] + \
               [("logits", b), ("places", b), ("gates", b), ("bias_out", b)]

    def experts(b):
        out = []
        for e in range(E):
            out += [("hidden", b, e, m) for m in range(M)]
            if e > 0:
                out.append(("expert_out", b, e - 1))
        return out + [("expert_out", b, E - 1)]

    def flat(groups):
        return [s for g in groups for s in g]

    plan = [("norm1", 0), ("turn1", 0), ("qkv", 0), ("sizes", 0)] + [("spread1", 0, g) for g in range(G)] + \
           [("flag", 0), ("guard", 0)]
    early = [[("norm1", 1)], [("vectors",)], [("turn1", 1)], [("qkv", 1)], [("context",)], [("sizes", 1)]] + \
            [[("spread1", 1, g)] for g in range(G)] + [[("flag", 1)]]
    plan += flat(weave(attention(0), early, 1))
    second = attention(1)
    plan += [("guard", 1)]
    chain = [[s] for s in after_attention(0) + cross(0) + router(0)]
    plan += flat(weave(chain, second, 1))
    first = experts(0)
    plan += flat(weave(second, [[s] for s in first], 3)) if second else []
    done = len([s for s in plan if s[0] in ("hidden", "expert_out")])
    rest = [[s] for s in first[done:]]
    plan += flat(weave([[s] for s in after_attention(1) + cross(1) + router(1)], rest, 1))
    plan += flat(rest)
    return plan + experts(1)


BANKS = {
    "vectors": ["vecT"], "turn1": ["xT"], "qkv": ["q", "k", "v"], "spread1": ["sq", "sk"], "sizes": ["size"],
    "flag": ["flag"], "context": ["cT", "k2", "sk2_0", "sk2_1", "sk2_2", "sk2_3", "v2a", "v2b"],
    "heads1": ["oT"], "joined": ["aT"], "project": ["proj"], "turn2": ["x2T"], "query2": ["q2"], "spread2": ["sq2"],
    "heads2": ["oT2"], "turn3": ["x3T"], "router_hidden": ["r"], "logits": ["lg"],
    "places": ["pos"], "gates": ["gT"], "bias_out": ["b2"], "hidden": ["h"], "expert_out": ["y"],
}


def build(nc, x, ctx_in, w_qkv, w_proj, wq, rw1, rw2, ew1, ew2, eb2, wkv, vectors, rows, c_bias, c_full, c_half,
          out):
    plan = schedule()
    use = {}
    for step in plan:
        for name in BANKS.get(step[0], []):
            use[(name, *step[1:])] = len(use)
    score_no = {}
    slot_no = {}
    group_no = {}
    slot2_no = {}
    group2_no = {}
    scores_before = {}
    hi_after = {}
    squares_no = {}
    rounded = 0
    normed_tiles = 0
    normed_after = {}
    for step in plan:
        if step[0] in ("norm1", "norm2", "norm3"):
            normed_tiles += TT
            normed_after[({"norm1": "xT", "norm2": "x2T", "norm3": "x3T"}[step[0]], step[1])] = normed_tiles
        if step[0] == "context":
            normed_tiles += 4
            normed_after["context"] = normed_tiles
        rounded += {"qkv": 2, "context": 1, "query2": 1}.get(step[0], 0)
        if step[0] == "sizes":
            squares_no[step[1]] = len(squares_no)
            hi_after[step[1]] = rounded
        if step[0] == "guard":
            scores_before[step[1]] = len(score_no)
        if step[0] == "scores1":
            slot_no[step[1:]] = len(slot_no)
            for j in range(HG):
                score_no[(*step[1:], j)] = len(score_no)
        if step[0] == "scores2":
            slot2_no[step[1:]] = len(slot2_no)
            for j in range(HG + 1):
                score_no[(*step[1:], "x", j)] = len(score_no)
        if step[0] == "out1":
            group_no[step[1:]] = len(group_no)
        if step[0] == "out2":
            group2_no[step[1:]] = len(group2_no)

    with ExitStack() as stack:
        def sb(name, shape, dt=F32):
            return stack.enter_context(nc.sbuf_tensor(name, shape, dt))

        def sem(name):
            return stack.enter_context(nc.semaphore(name))

        wqkv_s = sb("wqkv_s", [P, 3 * D])
        wproj_s = sb("wproj_s", [P, D])
        wq_s = sb("wq_s", [P, D])
        wkv_s = sb("wkv_s", [CD, 2 * D])
        wk_s, wv_s = wkv_s[:, 0:D], wkv_s[:, D:2 * D]
        rw1_s = sb("rw1_s", [P, F])
        rw2_s = sb("rw2_s", [P, M, E])
        ew1_s = sb("ew1_s", [P, E, F])
        ew2_s = sb("ew2_s", [P, E, M, D])
        eb2_s = sb("eb2_s", [E, D])
        rows_s = sb("rows_s", [P, 2 * D + E])
        bproj_s, bv_s, rb2_s = rows_s[:, 0:D], rows_s[:, D:2 * D], rows_s[:, 2 * D:2 * D + E]
        vec_s = sb("vec_s", [VROWS, P])
        col_s = sb("col_s", [P, VROWS])
        bias_s = sb("bias_s", [P, KC, L])
        full_s = sb("full_s", [P, P + E + 1])
        ident_s, iota_s, shift_s = full_s[:, 0:P], full_s[:, P:P + E], full_s[:, P + E:P + E + 1]
        half_s = sb("half_s", [P, 6 * P + 32], F16)
        spread_s = half_s[:, 0:4 * P].rearrange("p (k c) -> p k c", k=4)
        count_s = half_s[:, 4 * P:6 * P].rearrange("p (k c) -> p k c", k=2)
        size_s = half_s[:, 6 * P:6 * P + 32]
        ones_s = sb("ones_s", [64, 1])
        x_s = sb("x_s", [P, NT, D])
        xn_s = sb("xn_s", [P, NT, D])
        xT_s = sb("xT_s", [P, B * L])
        stats_s = sb("stats_s", [P, NT + 4, 6])
        mv_s = sb("mv_s", [P, NT + 4, 2])
        rstd_s = sb("rstd_s", [P, NT + 4, 4])
        qhi_s = sb("qhi_s", [P, B, L], F16)
        qlo_s = sb("qlo_s", [P, B, L], F16)
        khi_s = sb("khi_s", [P, B, L], F16)
        klo_s = sb("klo_s", [P, B, L], F16)
        sq_s = sb("sq_s", [P, B, 2, L], BF16)
        size_max_s = sb("size_max_s", [64, 2 * B])
        large_s = sb("large_s", [64, 2 * B])
        flag_s = sb("flag_s", [1, 2 * B], I32)
        max_s = sb("max_s", [P, TT, H])
        maxhi_s = sb("maxhi_s", [H, L], F16)
        maxlo_s = sb("maxlo_s", [H, L], F16)
        q16_s = sb("q16_s", [P, B, G, L], F16)
        k16_s = sb("k16_s", [P, B, G, L], F16)
        kz_s = sb("kz_s", [P, 2, HG, L], F16)
        v_s = sb("v_s", [P, B, KC, H, 32])
        prob_s = sb("prob_s", [P, NP, HG, L])
        prob2_s = sb("prob2_s", [P, NP, HG, L])
        probb_s = sb("probb_s", [P, 2, L])
        o_s = sb("o_s", [P, 2, L])
        o2_s = sb("o2_s", [P, 2, L])
        rden_s = sb("rden_s", [P, 2, B * G, TT, HG])
        att_s = xn_s[:, :, :].rearrange("p (b t) d -> p b t d", b=B)
        x1_s = sb("x1_s", [P, NT, D])
        ctx_s = sb("ctx_s", [P, B, 2, CD])
        ctxT_s = sb("ctxT_s", [CD, B, CW])
        ctxT4_s = sb("ctxT4_s", [CD, B, HG, 32])
        k2hi_s = sb("k2hi_s", [P, B, CW], F16)
        k2lo_s = sb("k2lo_s", [P, B, CW], F16)
        k2_s = sb("k2_s", [P, G, B, CW], F16)
        v2a_s = sb("v2a_s", [P, B, H, 32])
        v2b_s = sb("v2b_s", [P, B, H, 32])
        top_s = sb("top_s", [P, NT, 8])
        topi_s = sb("topi_s", [P, NT, 8], U32)
        topf_s = sb("topf_s", [P, NT, 2])
        lg_s = sb("lg_s", [P, NT, E])
        pick_s = sb("pick_s", [P, NT, 2, E])
        picks_s = sb("picks_s", [P, NT, E], F16)
        pr_s = sb("pr_s", [P, NT, 4])
        gate_s = sb("gate_s", [P, NT, E])
        gate2_s = sb("gate2_s", [P, NT, 2, E])
        keep_s = sb("keep_s", [P, NT, E])
        gateT_s = sb("gateT_s", [E, B, L])
        rT_s = prob2_s[:, 0, :, :]
        hT_s = sb("hT_s", [P, 2, M, L])

        bank = [stack.enter_context(nc.psum_tensor(f"bank{i}", [P, 512], F32)) for i in range(NB)]
        sbank = [stack.enter_context(nc.psum_tensor(f"sbank{i}", [P, 512], F32)) for i in range(NS)]
        obank = stack.enter_context(nc.psum_tensor("obank", [P, 512], F32))
        obank2 = stack.enter_context(nc.psum_tensor("obank2", [P, 512], F32))

        in_x = sem("in_x")
        in_first = sem("in_first")
        in_attn = sem("in_attn")
        in_ctx = sem("in_ctx")
        in_cross = sem("in_cross")
        in_router = sem("in_router")
        in_e1 = [sem(f"in_e1_{e}") for e in range(E)]
        in_e2 = [sem(f"in_e2_{e}") for e in range(E)]
        full = [sem(f"bank_full{i}") for i in range(NB)]
        moved = [sem(f"bank_moved{i}") for i in range(NB)]
        s_full = [sem(f"scores_full{i}") for i in range(NS)]
        s_moved = [sem(f"scores_moved{i}") for i in range(NS)]
        hi_done = sem("hi_done")
        biased = sem("biased")
        slot_used = sem("slot_used")
        slot2_used = sem("slot2_used")
        squared = sem("squared")
        kz_zero = sem("kz_zero")
        kz_ready = [sem(f"kz_ready{i}") for i in range(2)]
        size_done = sem("size_done")
        row_full = [sem(f"row_scores_full{i}") for i in range(2 * B)]
        row_max = [sem(f"row_max_done{i}") for i in range(2 * B)]
        turned = [sem(f"row_max_turned{i}") for i in range(2 * B)]
        halves = [sem(f"row_max_halves{i}") for i in range(2 * B)]
        shifted = [sem(f"row_max_in_place{i}") for i in range(2 * B)]
        o_moved = sem("o_moved")
        o2_moved = sem("o2_moved")
        zeroed = sem("zeroed")
        ones_done = sem("ones_done")
        pads = sem("pads")
        xb_done = sem("xb_done")
        stats_done = sem("stats_done")
        aggr_done = sem("aggr_done")
        rstd_done = sem("rstd_done")
        var_done = sem("var_done")
        root_done = sem("root_done")
        xn_done = sem("xn_done")
        den_done = sem("den_done")
        den2_done = sem("den2_done")
        x2_done = sem("x2_done")
        route_done = sem("route_done")
        exp_done = sem("exp_done")
        pick_done = sem("pick_done")
        gate_done = sem("gate_done")
        stored = sem("stored")

        def bank_of(key):
            return bank[use[key] % NB]

        def take(pe, key):
            n = use[key]
            if n >= NB:
                pe.wait_ge(moved[n % NB], n // NB)
            return bank[n % NB]

        def filled(key):
            return full[use[key] % NB]

        def wait_full(eng, key):
            n = use[key]
            eng.wait_ge(full[n % NB], n // NB + 1)
            return bank[n % NB]

        def emptied(key):
            return moved[use[key] % NB]

        def wait_moved(eng, key):
            n = use[key]
            eng.wait_ge(moved[n % NB], n // NB + 1)

        def tiles(b):
            return slice(b * TT, (b + 1) * TT)

        def too_large(eng, call):
            wait_moved(eng, ("flag", call))
            return eng.value_load(flag_s[0:1, call:call + 1], min_val=0, max_val=64)

        def operands(call):
            b = call % B
            if call < B:
                return lambda r, g: q16_s[r, b, g, :], lambda r, g: k16_s[r, b, g, :], L
            return lambda r, g: q16_s[r, b, g, :], lambda r, g: k2_s[r, g, b, 0:NC], NC

        block = stack.enter_context(nc.Block())

        @block.sync
        def _(sp):
            sp.dma_start(x_s[:, 0:TT, :], x[0].rearrange("(t p) d -> p t d", p=P)).then_inc(in_x, 16)
            sp.dma_start(wqkv_s[:, :], w_qkv).then_inc(in_first, 16)
            sp.dma_start(half_s[:, :], c_half).then_inc(in_first, 16)
            sp.dma_start(x_s[:, TT:NT, :], x[1].rearrange("(t p) d -> p t d", p=P)).then_inc(in_x, 16)
            sp.dma_start(bias_s[:, :, :], c_bias).then_inc(in_attn, 16)
            sp.dma_start(vec_s[:, :], vectors).then_inc(in_ctx, 16)
            sp.dma_start(ctx_s[:, :, 0, :], ctx_in[:, 0:P, :].rearrange("b k c -> k b c")).then_inc(in_ctx, 16)
            sp.dma_start(ctx_s[0:NCB, :, 1, :], ctx_in[:, P:NC, :].rearrange("b k c -> k b c")).then_inc(in_ctx, 16)
            sp.dma_start(rows_s[:, :], rows.partition_broadcast(P)).then_inc(in_cross, 16)
            sp.dma_start(wkv_s[:, :], wkv).then_inc(in_cross, 16)
            sp.dma_start(wproj_s[:, :], w_proj).then_inc(in_cross, 16)
            sp.dma_start(wq_s[:, :], wq).then_inc(in_cross, 16)
            sp.dma_start(rw1_s[:, :], rw1).then_inc(in_router, 16)
            sp.dma_start(rw2_s[:, :, :], rw2.rearrange("(m p) e -> p m e", p=P)).then_inc(in_router, 16)
            sp.dma_start(eb2_s[:, :], eb2).then_inc(in_router, 16)
            for e in range(E):
                sp.dma_start(ew1_s[:, e, :], ew1[e]).then_inc(in_e1[e], 16)
                sp.dma_start(ew2_s[:, e, :, :], ew2[e].rearrange("(m p) c -> p m c", p=P)).then_inc(in_e2[e], 16)
            def place_keys(n):
                b, g = divmod(n, G)
                wait_moved(sp, ("sk", b, g))
                if n >= 2:
                    last = score_no[(*divmod(n - 2, G), KC - 1, HG - 1)]
                    sp.wait_ge(s_full[last % NS], last // NS + 1)
                for j in range(HG):
                    r = slice(32 * j, 32 * j + 32)
                    sp.dma_start(kz_s[r, n % 2, j, :], k16_s[r, b, g, :]).then_inc(kz_ready[n % 2], 16)

            sp.wait_ge(kz_zero, 1)
            for step in plan:
                if step[0] == "spread1" and step[1:] == (0, 0):
                    place_keys(0)
                if step[0] == "scores1" and step[3] == 0 and step[1:3] != (B - 1, G - 1):
                    place_keys(step[1] * G + step[2] + 1)
                if step[0] == "guard":
                    call = step[1]
                    with sp.If(too_large(sp, call) > 0):
                        sp.wait_ge(halves[call], 2)
                        for part, half in enumerate((maxhi_s, maxlo_s)):
                            for g in range(G):
                                for j in range(HG):
                                    p = 32 * j + 3 * DH + part
                                    sp.dma_start(q16_s[p:p + 1, call % B, g, :],
                                                 half[HG * g + j:HG * g + j + 1, :]).then_inc(shifted[call], 16)
                if step[0] != "expert_out" or step[2] != E - 1:
                    continue
                b = step[1]
                wait_moved(sp, ("y", b, E - 1))
                sp.dma_start(out[b].rearrange("(t p) d -> p t d", p=P), x1_s[:, tiles(b), :]).then_inc(stored, 16)
            sp.wait_ge(stored, 16 * B)

        @block.gpsimd
        def _(pool):
            pool.memset(kz_s[:, :, :, :], 0.0).then_inc(kz_zero, 1)
            pool.memset(ones_s[:, :], 1.0).then_inc(ones_done, 1)
            pool.memset(v_s[:, :, :, :, DH:32], 0.0).then_inc(zeroed, 1)
            pool.memset(v2a_s[:, :, :, DH:32], 0.0).then_inc(zeroed, 1)
            pool.memset(v2b_s[:, :, :, DH:32], 0.0).then_inc(zeroed, 1)
            pool.memset(mv_s[:, NT:NT + 4, :], 1.0).then_inc(pads, 1)
            pool.memset(ctxT4_s[:, :, :, :], 0.0).then_inc(pads, 1)
            pool.memset(ctxT_s[:, :, :], 0.0).then_inc(pads, 1)
            pool.memset(k2hi_s[:, :, :], 0.0).then_inc(pads, 1)
            pool.memset(k2lo_s[:, :, :], 0.0).then_inc(pads, 1)
            pool.wait_ge(zeroed, 3)
            pool.memset(v_s[:, :, :, :, DH:DH + 1], 1.0).then_inc(zeroed, 1)
            pool.memset(v2a_s[:, :, :, DH:DH + 1], 1.0).then_inc(zeroed, 1)
            pool.memset(v2b_s[:, :, :, DH:DH + 1], 1.0).then_inc(zeroed, 1)
            def squares(call):
                b = call % B
                pool.wait_ge(hi_done, hi_after[call])
                pool.tensor_tensor(sq_s[:, call % B, 0, :], qhi_s[:, b, :], qhi_s[:, b, :], ALU.mult).then_inc(squared, 1)
                k, n = (khi_s[:, b, :], L) if call < B else (k2hi_s[:, b, 0:NC], NC)
                pool.tensor_tensor(sq_s[:, call % B, 1, 0:n], k, k, ALU.mult).then_inc(squared, 1)

            squares(0)
            pool.wait_ge(in_x, 32)
            pool.wait_ge(in_cross, 16 * 4)
            def add_bias(b):
                pool.wait_ge(xn_done, normed_after[("xT", b)])
                for t in range(b * TT, (b + 1) * TT):
                    pool.tensor_tensor(x_s[:, t, :], x_s[:, t, :], bproj_s, ALU.add).then_inc(xb_done, 1)

            add_bias(0)
            for step in plan:
                if step == ("turn1", 1):
                    add_bias(1)
                if step[0] == "sizes" and step[1] > 0:
                    squares(step[1])

        @block.scalar
        def _(act):
            act.dma_start(full_s[:, :], c_full).then_inc(in_first, 16)
            act.preload_act_table_set("natural_log_exp_and_others")

            COL = {"eb1": 0, "rb1": E * M, "norm_g": E * M + M, "norm_b": E * M + M + 1,
                   "bq": E * M + M + 2, "bk": E * M + M + 3}

            def column(name, i=0):
                return col_s[:, COL[name] + i:COL[name] + i + 1]

            def move(key, dst, src, func=ACT.Copy, **kw):
                wait_full(act, key)
                act.activation(dst, src, func, **kw).then_inc(emptied(key), 1)

            roots = 0

            def root(ts):
                act.wait_ge(var_done, roots + 1)
                act.activation(rstd_s[:, ts, 1], rstd_s[:, ts, 0], ACT.Ln).then_inc(root_done, 1)
                act.wait_ge(root_done, 2 * roots + 1)
                act.activation(rstd_s[:, ts, 2], rstd_s[:, ts, 1], ACT.Exp, scale=-0.5).then_inc(root_done, 1)
                return roots + 1

            for step in plan:
                stage, arg = step[0], step[1:]
                if stage in ("norm1", "norm2", "norm3"):
                    roots = root(tiles(*arg))
                elif stage == "context":
                    roots = root(slice(NT, NT + 4))
                if stage == "vectors":
                    move(("vecT",), col_s[:, 0:VROWS], bank_of(("vecT",))[:, 0:VROWS])
                elif stage == "turn1":
                    b, = arg
                    move(("xT", b), xT_s[:, b * L:(b + 1) * L], bank_of(("xT", b))[:, :])
                elif stage == "qkv":
                    b, = arg
                    for key, hi in (("q", qhi_s), ("k", khi_s)):
                        ps = wait_full(act, (key, b))
                        act.activation(hi[:, b, :], ps[:, :], ACT.Copy).then_inc(hi_done, 1)
                    ps = bank_of(("v", b))
                    act.wait_ge(zeroed, 4)
                    move(("v", b), v_s[:, b, :, :, 0:DH], ps[:, :].rearrange("p (c h d) -> p c h d", c=KC, h=H))
                elif stage == "spread1":
                    b, g = arg
                    move(("sq", b, g), q16_s[:, b, g, :], bank_of(("sq", b, g))[:, :])
                elif stage == "context":
                    ps = wait_full(act, ("k2",))
                    act.wait_ge(pads, 5)
                    wait_moved(act, ("vecT",))
                    act.activation(k2hi_s[:, :, 0:NC], ps[:, 0:B * CW].rearrange("p (b k) -> p b k", b=B)[:, :, 0:NC],
                                   ACT.Identity, bias=column("bk")).then_inc(hi_done, 1)
                    act.wait_ge(in_first, 16 * 3)
                    for g in range(G):
                        move((f"sk2_{g}",), k2_s[:, g, :, :],
                             bank_of((f"sk2_{g}",))[:, 0:B * CW].rearrange("p (b k) -> p b k", b=B),
                             ACT.Identity, bias=shift_s[:, 0:1])
                elif stage == "scores1":
                    b, g, c = arg
                    slot = slot_no[arg]
                    if slot >= NP:
                        act.wait_ge(slot_used, slot - NP + 1)
                    for j in range(HG):
                        n = score_no[(*arg, j)]
                        act.wait_ge(s_full[n % NS], n // NS + 1)
                        act.activation(prob_s[:, slot % NP, j, :], sbank[n % NS][:, :], ACT.Exp,
                                       scale=SCALE).then_inc(s_moved[n % NS], 1)
                elif stage == "scores2":
                    slot = slot2_no[arg]
                    if arg[0] > 0 and arg[1] == 0:
                        wait_full(act, ("lg", arg[0] - 1))
                    if slot >= NP:
                        act.wait_ge(slot2_used, slot - NP + 1)
                    for j in range(HG + 1):
                        n = score_no[(*arg, "x", j)]
                        act.wait_ge(s_full[n % NS], n // NS + 1)
                        dst = prob2_s[:, slot % NP, j, :] if j < HG else probb_s[:, slot % 2, :]
                        act.activation(dst, sbank[n % NS][:, :], ACT.Exp,
                                       scale=SCALE).then_inc(s_moved[n % NS], 1)
                elif stage == "out1":
                    b, g = arg
                    n = group_no[arg]
                    act.wait_ge(slot_used, slot_no[(b, g, KC - 1)] + 1)
                    if n >= 2:
                        wait_full(act, ("oT", *divmod(n - 2, G)))
                    act.activation(o_s[:, n % 2, :], obank[:, :], ACT.Copy).then_inc(o_moved, 1)
                elif stage == "out2":
                    n = group2_no[arg]
                    act.wait_ge(slot2_used, slot2_no[arg] + 1)
                    if n >= 2:
                        wait_full(act, ("oT2", *divmod(n - 2, G)))
                    act.activation(o2_s[:, n % 2, :], obank2[:, :], ACT.Copy).then_inc(o2_moved, 1)
                elif stage == "joined":
                    b, = arg
                    move(("aT", b), xT_s[:, b * L:(b + 1) * L], bank_of(("aT", b))[:, :])
                elif stage == "query2":
                    b, = arg
                    ps = wait_full(act, ("q2", b))
                    act.activation(qhi_s[:, b, :], ps[:, :], ACT.Identity, bias=column("bq")).then_inc(hi_done, 1)
                elif stage == "spread2":
                    b, g = arg
                    move(("sq2", b, g), q16_s[:, b, g, :], bank_of(("sq2", b, g))[:, :])
                elif stage == "turn3":
                    b, = arg
                    move(("x3T", b), xT_s[:, b * L:(b + 1) * L], bank_of(("x3T", b))[:, :])
                elif stage == "router_hidden":
                    b, m = arg
                    move(("r", b, m), rT_s[:, m, :], bank_of(("r", b, m))[:, :], ACT.Relu, bias=column("rb1", m))
                elif stage == "places":
                    b, = arg
                    act.wait_ge(route_done, b + 1)
                    act.activation(pr_s[:, tiles(b), 1], pr_s[:, tiles(b), 0], ACT.Exp).then_inc(exp_done, 1)
                elif stage == "gates":
                    b, = arg
                    move(("gT", b), gateT_s[:, b, :], bank_of(("gT", b))[0:E, :])
                elif stage == "hidden":
                    b, e, m = arg
                    i = b * E + e
                    if i >= 2 and m == 0:
                        wait_full(act, ("y", (i - 2) // E, (i - 2) % E))
                    move(("h", b, e, m), hT_s[:, i % 2, m, :], bank_of(("h", b, e, m))[:, :], ACT.Relu,
                         bias=column("eb1", e * M + m))

        @block.vector
        def _(dve):
            counts = {"stats": 0, "aggr": 0, "rstd": 0, "root": 0, "hi": 0, "pick": 0, "gate": 0}

            def mean_var(src, rows, where):
                for i, s in enumerate(src):
                    dve.bn_stats(stats_s[0:rows[i], where + i, :], s).then_inc(stats_done, 1)
                counts["stats"] += len(src)
                dve.wait_ge(stats_done, counts["stats"])
                for i in range(len(src)):
                    dve.bn_aggr(mv_s[0:rows[i], where + i, :], stats_s[0:rows[i], where + i, :]).then_inc(aggr_done, 1)
                counts["aggr"] += len(src)
                dve.wait_ge(aggr_done, counts["aggr"])

            def step_rstd(ins):
                ins.then_inc(rstd_done, 1)
                counts["rstd"] += 1
                dve.wait_ge(rstd_done, counts["rstd"])

            def rsqrt(ts, mul, add):
                step = counts["root"]
                counts["root"] += 1
                dve.tensor_scalar(rstd_s[:, ts, 0], mv_s[:, ts, 1], mul, add, ALU.mult, ALU.add).then_inc(var_done, 1)
                dve.wait_ge(root_done, 2 * step + 2)
                r = rstd_s[:, ts, 2]
                step_rstd(dve.tensor_tensor(rstd_s[:, ts, 1], r, r, ALU.mult))
                step_rstd(dve.scalar_tensor_tensor(out=rstd_s[:, ts, 3], in0=rstd_s[:, ts, 1], scalar=-0.5,
                                                   in1=rstd_s[:, ts, 0], op0=ALU.mult, op1=ALU.mult))
                step_rstd(dve.scalar_tensor_tensor(out=r, in0=rstd_s[:, ts, 3], scalar=1.5, in1=r,
                                                   op0=ALU.add, op1=ALU.mult))

            def layernorm(b, src, mul=1.0, add=EPS):
                ts = tiles(b)
                mean_var([src[:, t, :] for t in range(ts.start, ts.stop)], [P] * TT, ts.start)
                rsqrt(ts, mul, add)
                for t in range(ts.start, ts.stop):
                    dve.tensor_scalar(xn_s[:, t, :], src[:, t, :], mv_s[:, t, 0:1], rstd_s[:, t, 2:3],
                                      ALU.subtract, ALU.mult).then_inc(xn_done, 1)

            def heads(key, kind, den, n, b, g):
                ps = wait_full(dve, (key, b, g))[:, :].rearrange("p (t j r) -> p t j r", t=TT, j=HG)
                dve.reciprocal(rden_s[:, kind, n, :, :], ps[:, :, :, DH]).then_inc(den, 1)
                dve.wait_ge(den, n + 1)
                dst = att_s[:, b, :, g * 32:(g + 1) * 32].rearrange("p t (j d) -> p t j d", j=HG)
                dve.tensor_tensor(dst, ps[:, :, :, 0:DH], rden_s[:, kind, n, :, :].unsqueeze(3).to_broadcast([P, TT, HG, DH]),
                                  ALU.mult).then_inc(emptied((key, b, g)), 1)

            def pick_step(ins):
                ins.then_inc(pick_done, 1)
                counts["pick"] += 1
                dve.wait_ge(pick_done, counts["pick"])

            def gate_step(ins):
                ins.then_inc(gate_done, 1)
                counts["gate"] += 1
                dve.wait_ge(gate_done, counts["gate"])

            for step in plan:
                stage, arg = step[0], step[1:]
                if stage == "norm1":
                    b, = arg
                    dve.wait_ge(in_x, 16 * 2)
                    if b == 0:
                        dve.wait_ge(in_first, 16 * 3)
                    layernorm(b, x_s)
                elif stage == "qkv":
                    b, = arg
                    for key, hi, lo in (("q", qhi_s, qlo_s), ("k", khi_s, klo_s)):
                        counts["hi"] += 1
                        dve.wait_ge(hi_done, counts["hi"])
                        dve.tensor_tensor(lo[:, b, :], bank_of((key, b))[:, :], hi[:, b, :],
                                          ALU.subtract).then_inc(emptied((key, b)), 1)
                elif stage == "spread1":
                    b, g = arg
                    ps = wait_full(dve, ("sk", b, g))
                    dve.tensor_scalar(k16_s[:, b, g, :], ps[:, :], shift_s[:, 0:1], None,
                                      ALU.add).then_inc(emptied(("sk", b, g)), 1)
                elif stage == "sizes":
                    call, = arg
                    ps = wait_full(dve, ("size", call))
                    if call < B:
                        dve.tensor_reduce(size_max_s[:, call:call + 1], ps[0:64, :], AX.X, ALU.max).then_inc(size_done, 1)
                    else:
                        dve.tensor_reduce(size_max_s[0:32, call:call + 1], ps[0:32, :], AX.X, ALU.max)
                        dve.tensor_reduce(size_max_s[32:64, call:call + 1], ps[32:64, 0:NC], AX.X,
                                          ALU.max).then_inc(size_done, 1)
                    dve.wait_ge(size_done, squares_no[call] + 1)
                    dve.tensor_scalar(large_s[:, call:call + 1], size_max_s[:, call:call + 1], LIMIT / SCALE, None,
                                      ALU.is_gt).then_inc(emptied(("size", call)), 1)
                elif stage == "flag":
                    call, = arg
                    ps = wait_full(dve, ("flag", call))
                    dve.tensor_copy(flag_s[0:1, call:call + 1], ps[0:1, 0:1]).then_inc(emptied(("flag", call)), 1)
                elif stage == "guard":
                    call, = arg
                    n = operands(call)[2]
                    with dve.If(too_large(dve, call) > 0):
                        for i in range(H * TT):
                            h, t = divmod(i, TT)
                            dve.wait_ge(row_full[call], i + 1)
                            dve.tensor_reduce(max_s[:, t, h:h + 1], sbank[i % 2][:, 0:n], AX.X,
                                              ALU.max).then_inc(row_max[call], 1)
                        dve.wait_ge(turned[call], 1)
                        dve.tensor_scalar(maxhi_s[:, :], sbank[2][0:H, :], 1.0 / SHIFT, None,
                                          ALU.mult).then_inc(halves[call], 1)
                        dve.wait_ge(halves[call], 1)
                        dve.scalar_tensor_tensor(out=maxlo_s[:, :], in0=sbank[2][0:H, :], scalar=1.0 / SHIFT,
                                                 in1=maxhi_s[:, :], op0=ALU.mult,
                                                 op1=ALU.subtract).then_inc(halves[call], 1)
                elif stage == "context":
                    dve.wait_ge(in_ctx, 16 * 3)
                    rows = [P, NCB, P, NCB]
                    src = [ctx_s[0:rows[i], i // 2, i % 2, :] for i in range(4)]
                    dve.wait_ge(pads, 1)
                    mean_var(src, rows, NT)
                    rsqrt(slice(NT, NT + 4), 1.0, EPS)
                    for i in range(4):
                        r = rows[i]
                        dve.tensor_scalar(src[i], src[i], mv_s[0:r, NT + i, 0:1], rstd_s[0:r, NT + i, 2:3],
                                          ALU.subtract, ALU.mult).then_inc(xn_done, 1)
                    ps = wait_full(dve, ("cT",))[0:CD, 0:B * CW].rearrange("p (b k) -> p b k", b=B)
                    dve.wait_ge(pads, 3)
                    wait_moved(dve, ("vecT",))
                    tg = E * M + M + 4
                    counts["rstd"] += 1
                    dve.tensor_scalar(ctxT_s[:, :, 0:NC], ps[:, :, 0:NC], col_s[0:CD, tg:tg + 1],
                                      col_s[0:CD, tg + 1:tg + 2], ALU.mult, ALU.add).then_inc(rstd_done, 1)
                    dve.wait_ge(rstd_done, counts["rstd"])
                    for b in range(B):
                        ins = dve.tensor_copy(ctxT4_s[:, b, :, 0:NCB],
                                              ctxT_s[:, b:b + 1, P:NC].to_broadcast([CD, HG, NCB]))
                    ins.then_inc(emptied(("cT",)), 1)
                    counts["hi"] += 1
                    dve.wait_ge(hi_done, counts["hi"])
                    bkc = E * M + M + 3
                    ps = bank_of(("k2",))[:, 0:B * CW].rearrange("p (b k) -> p b k", b=B)[:, :, 0:NC]
                    dve.scalar_tensor_tensor(out=k2lo_s[:, :, 0:NC], in0=ps, scalar=col_s[:, bkc:bkc + 1],
                                             in1=k2hi_s[:, :, 0:NC], op0=ALU.add,
                                             op1=ALU.subtract).then_inc(emptied(("k2",)), 1)
                    dve.wait_ge(zeroed, 6)
                    dve.wait_ge(in_cross, 16 * 4)
                    for key, dst in (("v2a", v2a_s), ("v2b", v2b_s)):
                        ps = wait_full(dve, (key,))
                        for b in range(B):
                            ins = dve.tensor_tensor(dst[:, b, :, 0:DH],
                                                    ps[:, b * D:(b + 1) * D].rearrange("p (h d) -> p h d", h=H),
                                                    bv_s.rearrange("p (h d) -> p h d", h=H), ALU.add)
                        ins.then_inc(emptied((key,)), 1)
                elif stage == "scores1":
                    b, g, c = arg
                    slot = slot_no[arg]
                    if slot == 0:
                        dve.wait_ge(in_attn, 16)
                    for pair in range(2):
                        n = score_no[(*arg, 2 * pair + 1)]
                        dve.wait_ge(s_moved[(n - 1) % NS], (n - 1) // NS + 1)
                        dve.wait_ge(s_moved[n % NS], n // NS + 1)
                        pr = prob_s[:, slot % NP, 2 * pair:2 * pair + 2, :]
                        dve.tensor_tensor(pr, pr, bias_s[:, c:c + 1, :].to_broadcast([P, 2, L]),
                                          ALU.mult).then_inc(biased, 1)
                elif stage == "heads1":
                    b, g = arg
                    heads("oT", 0, den_done, group_no[arg], b, g)
                elif stage == "heads2":
                    b, g = arg
                    heads("oT2", 1, den2_done, group2_no[arg], b, g)
                    if g == G - 1:
                        wait_moved(dve, ("oT2", b, g))
                        dve.tensor_tensor(x1_s[:, tiles(b), :], x1_s[:, tiles(b), :], att_s[:, b, :, :],
                                          ALU.add).then_inc(x2_done, 1)
                elif stage == "project":
                    b, = arg
                    ps = wait_full(dve, ("proj", b))
                    dve.wait_ge(xb_done, (b + 1) * TT)
                    dve.tensor_tensor(x1_s[:, tiles(b), :], ps[:, :].rearrange("p (t d) -> p t d", t=TT),
                                      x_s[:, tiles(b), :], ALU.add).then_inc(emptied(("proj", b)), 1)
                elif stage == "norm2":
                    b, = arg
                    wait_moved(dve, ("proj", b))
                    layernorm(b, x1_s, 1.0 + EPS, EPS * EPS)
                elif stage == "turn2":
                    b, = arg
                    ps = wait_full(dve, ("x2T", b))
                    gc = E * M + M
                    dve.tensor_scalar(xT_s[:, b * L:(b + 1) * L], ps[:, :], col_s[:, gc:gc + 1], col_s[:, gc + 1:gc + 2],
                                      ALU.mult, ALU.add).then_inc(emptied(("x2T", b)), 1)
                elif stage == "query2":
                    b, = arg
                    gc = E * M + M
                    counts["hi"] += 1
                    dve.wait_ge(hi_done, counts["hi"])
                    dve.scalar_tensor_tensor(out=qlo_s[:, b, :], in0=bank_of(("q2", b))[:, :],
                                             scalar=col_s[:, gc + 2:gc + 3], in1=qhi_s[:, b, :], op0=ALU.add,
                                             op1=ALU.subtract).then_inc(emptied(("q2", b)), 1)
                elif stage == "norm3":
                    b, = arg
                    dve.wait_ge(x2_done, b + 1)
                    layernorm(b, x1_s)
                elif stage == "logits":
                    b, = arg
                    ts = tiles(b)
                    ps = wait_full(dve, ("lg", b))
                    dve.tensor_tensor(lg_s[:, ts, :], ps[:, 0:TT * E].rearrange("p (t e) -> p t e", t=TT),
                                      rb2_s.unsqueeze(1).to_broadcast([P, TT, E]), ALU.add).then_inc(emptied(("lg", b)), 1)
                    wait_moved(dve, ("lg", b))
                    for t in range(ts.start, ts.stop):
                        ins = dve.max(top_s[:, t, :], lg_s[:, t, :])
                    pick_step(ins)
                    for t in range(ts.start, ts.stop):
                        ins = dve.max_index(topi_s[:, t, :], top_s[:, t, :], lg_s[:, t, :])
                    pick_step(ins)
                    dve.tensor_tensor(pr_s[:, ts, 0], top_s[:, ts, 1], top_s[:, ts, 0],
                                      ALU.subtract).then_inc(route_done, 1)
                    pick_step(dve.tensor_copy(topf_s[:, ts, :], topi_s[:, ts, 0:2]))
                    for k in range(2):
                        ins = dve.tensor_tensor(pick_s[:, ts, k, :], iota_s.unsqueeze(1).to_broadcast([P, TT, E]),
                                                topf_s[:, ts, k:k + 1].to_broadcast([P, TT, E]), ALU.is_equal)
                    pick_step(ins)
                    pick_step(dve.tensor_tensor(picks_s[:, ts, :], pick_s[:, ts, 0, :], pick_s[:, ts, 1, :], ALU.add))
                elif stage == "places":
                    b, = arg
                    ts = tiles(b)
                    dve.wait_ge(exp_done, b + 1)
                    gate_step(dve.tensor_scalar(pr_s[:, ts, 2], pr_s[:, ts, 1], 1.0, None, ALU.add))
                    gate_step(dve.reciprocal(pr_s[:, ts, 3], pr_s[:, ts, 2]))
                    gate_step(dve.tensor_tensor(pr_s[:, ts, 2], pr_s[:, ts, 1], pr_s[:, ts, 3], ALU.mult))
                    for k in range(2):
                        ins = dve.tensor_tensor(gate2_s[:, ts, k, :], pick_s[:, ts, k, :],
                                                pr_s[:, ts, 3 - k:4 - k].to_broadcast([P, TT, E]), ALU.mult)
                    gate_step(ins)
                    gate_step(dve.tensor_tensor(gate2_s[:, ts, 0, :], gate2_s[:, ts, 0, :], gate2_s[:, ts, 1, :], ALU.add))
                    ps = wait_full(dve, ("pos", b))
                    dve.tensor_scalar(keep_s[:, ts, :], ps[:, 0:TT * E].rearrange("p (t e) -> p t e", t=TT), float(CAP),
                                      None, ALU.is_lt).then_inc(emptied(("pos", b)), 1)
                    wait_moved(dve, ("pos", b))
                    gate_step(dve.tensor_tensor(gate_s[:, ts, :], gate2_s[:, ts, 0, :], keep_s[:, ts, :], ALU.mult))
                elif stage == "bias_out":
                    b, = arg
                    ps = wait_full(dve, ("b2", b))
                    dve.tensor_tensor(x1_s[:, tiles(b), :], ps[:, :].rearrange("p (t d) -> p t d", t=TT),
                                      x1_s[:, tiles(b), :], ALU.add).then_inc(emptied(("b2", b)), 1)
                elif stage == "expert_out":
                    b, e = arg
                    wait_moved(dve, ("b2", b) if e == 0 else ("y", b, e - 1))
                    ps = wait_full(dve, ("y", b, e))
                    for t in range(TT):
                        ins = dve.scalar_tensor_tensor(out=x1_s[:, b * TT + t, :], in0=ps[:, t * D:(t + 1) * D],
                                                       scalar=gate_s[:, b * TT + t, e:e + 1], in1=x1_s[:, b * TT + t, :],
                                                       op0=ALU.mult, op1=ALU.add)
                    ins.then_inc(emptied(("y", b, e)), 1)

        @block.tensor
        def _(pe):
            counts = {"xn": 0, "gate": 0, "pick": 0}

            def transposes(key, src, n=TT, rows=P):
                ps = take(pe, key)
                for t in range(n):
                    ins = pe.transpose(ps[0:rows, t * P:(t + 1) * P], src(t), ident_s)
                ins.then_inc(filled(key), 1)

            def normed(key, b):
                pe.wait_ge(xn_done, normed_after[key])
                transposes(key, lambda t: xn_s[:, b * TT + t, :])

            def spread(key, hi, lo, side, g):
                ps = take(pe, key)
                r = slice(32 * g, 32 * g + 32)
                n = hi.free_size()
                pe.matmul(ps[:, 0:n], spread_s[r, 2 * side, :], hi, start=True, stop=False)
                pe.matmul(ps[:, 0:n], spread_s[r, 2 * side + 1, :], lo, start=False, stop=True).then_inc(filled(key), 1)

            def next_scores(n):
                if n >= NS:
                    pe.wait_ge(s_moved[n % NS], n // NS)
                return sbank[n % NS]

            for step in plan:
                stage, arg = step[0], step[1:]
                if stage == "vectors":
                    pe.wait_ge(in_ctx, 16 * 3)
                    ps = take(pe, ("vecT",))
                    n = VROWS
                    pe.transpose(ps[:, 0:n], vec_s[0:n, :], ident_s[0:n, 0:n]).then_inc(filled(("vecT",)), 1)
                elif stage == "turn1":
                    if arg[0] == 0:
                        pe.wait_ge(in_first, 16 * 3)
                    normed(("xT", arg[0]), arg[0])
                elif stage == "qkv":
                    b, = arg
                    wait_moved(pe, ("xT", b))
                    for i, key in enumerate(("q", "k")):
                        ps = take(pe, (key, b))
                        pe.matmul(ps[:, :], wqkv_s[:, i * D:(i + 1) * D], xT_s[:, b * L:(b + 1) * L],
                                  start=True, stop=True).then_inc(filled((key, b)), 1)
                    ps = take(pe, ("v", b))
                    for t in range(TT):
                        ins = pe.matmul(ps[:, t * D:(t + 1) * D], xT_s[:, b * L + t * P:b * L + (t + 1) * P],
                                        wqkv_s[:, 2 * D:3 * D], start=True, stop=True)
                    ins.then_inc(filled(("v", b)), 1)
                elif stage == "spread1":
                    b, g = arg
                    r = slice(32 * g, 32 * g + 32)
                    wait_moved(pe, ("q", b))
                    spread(("sq", b, g), qhi_s[r, b, :], qlo_s[r, b, :], 0, g)
                    wait_moved(pe, ("k", b))
                    spread(("sk", b, g), khi_s[r, b, :], klo_s[r, b, :], 1, g)
                elif stage == "sizes":
                    call, = arg
                    n = L if call < B else NC
                    pe.wait_ge(squared, 2 * squares_no[call] + 2)
                    ps = take(pe, ("size", call))
                    pe.matmul(ps[0:32, :], size_s, sq_s[:, call % B, 0, :], start=True, stop=True)
                    pe.matmul(ps[32:64, 0:n], size_s, sq_s[:, call % B, 1, 0:n], start=True,
                              stop=True).then_inc(filled(("size", call)), 1)
                elif stage == "flag":
                    call, = arg
                    wait_moved(pe, ("size", call))
                    pe.wait_ge(ones_done, 1)
                    ps = take(pe, ("flag", call))
                    pe.matmul(ps[0:1, 0:1], large_s[:, call:call + 1], ones_s[:, :], start=True,
                              stop=True).then_inc(filled(("flag", call)), 1)
                elif stage == "guard":
                    call, = arg
                    queries, keys, n = operands(call)
                    with pe.If(too_large(pe, call) > 0):
                        for s in range(NS):
                            used = (scores_before[call] - s + NS - 1) // NS
                            if used > 0:
                                pe.wait_ge(s_moved[s], used)
                        for g in range(G):
                            wait_moved(pe, (("sq" if call < B else "sq2"), call % B, g))
                            wait_moved(pe, ("sk", call % B, g) if call < B else (f"sk2_{g}",))
                        for i in range(H * TT):
                            h, t = divmod(i, TT)
                            r = slice(32 * (h % HG), 32 * (h % HG) + 32)
                            if i >= 2:
                                pe.wait_ge(row_max[call], i - 1)
                            pe.matmul(sbank[i % 2][:, 0:n], queries(r, h // HG)[:, t * P:(t + 1) * P],
                                      keys(r, h // HG), start=True, stop=True).then_inc(row_full[call], 1)
                        pe.wait_ge(row_max[call], H * TT)
                        for t in range(TT):
                            ins = pe.transpose(sbank[2][0:H, t * P:(t + 1) * P], max_s[:, t, :], ident_s)
                        ins.then_inc(turned[call], 1)
                        pe.wait_ge(shifted[call], 16 * 2 * H)
                elif stage == "context":
                    pe.wait_ge(xn_done, normed_after["context"])
                    ps = take(pe, ("cT",))
                    for b in range(B):
                        pe.transpose(ps[0:CD, b * CW:b * CW + P], ctx_s[:, b, 0, :], ident_s)
                        ins = pe.transpose(ps[0:CD, b * CW + P:b * CW + NC], ctx_s[0:NCB, b, 1, :],
                                           ident_s[0:NCB, 0:NCB])
                    ins.then_inc(filled(("cT",)), 1)
                    wait_moved(pe, ("cT",))
                    pe.wait_ge(in_cross, 16 * 4)
                    ps = take(pe, ("k2",))
                    pe.matmul(ps[:, 0:B * CW], wk_s, ctxT_s[:, :, :], start=True, stop=True).then_inc(filled(("k2",)), 1)
                    wait_moved(pe, ("k2",))
                    for g in range(G):
                        r = slice(32 * g, 32 * g + 32)
                        spread((f"sk2_{g}",), k2hi_s[r, :, :], k2lo_s[r, :, :], 1, g)
                    for key, src in (("v2a", lambda b: ctxT_s[:, b, 0:P]), ("v2b", lambda b: ctxT4_s[:, b, :, :])):
                        ps = take(pe, (key,))
                        for b in range(B):
                            ins = pe.matmul(ps[:, b * D:(b + 1) * D], src(b), wv_s, start=True, stop=True)
                        ins.then_inc(filled((key,)), 1)
                elif stage == "scores1":
                    b, g, c = arg
                    wait_moved(pe, ("sq", b, g))
                    pe.wait_ge(kz_ready[g % 2], 16 * HG * ((b * G + g) // 2 + 1))
                    for j in range(HG):
                        n = score_no[(*arg, j)]
                        ps = next_scores(n)
                        pe.matmul(ps[:, :], kz_s[:, (b * G + g) % 2, j, c * P:(c + 1) * P], q16_s[:, b, g, :],
                                  start=True, stop=True).then_inc(s_full[n % NS], 1)
                elif stage == "values1":
                    b, g, c = arg
                    if c == 0:
                        wait_moved(pe, ("v", b))
                        n = group_no[(b, g)]
                        if n > 0:
                            pe.wait_ge(o_moved, n)
                    slot = slot_no[arg]
                    for j in range(HG):
                        if j % 2 == 0:
                            pe.wait_ge(biased, 2 * slot + j // 2 + 1)
                        ins = pe.matmul(obank[32 * j:32 * j + 32, :], v_s[:, b, c, HG * g + j, :],
                                        prob_s[:, slot % NP, j, :], start=(c == 0), stop=(c == KC - 1))
                    ins.then_inc(slot_used, 1)
                elif stage == "scores2":
                    b, g = arg
                    wait_moved(pe, ("sq2", b, g))
                    for j in range(HG):
                        n = score_no[(*arg, "x", j)]
                        r = slice(32 * j, 32 * j + 32)
                        ps = next_scores(n)
                        pe.matmul(ps[:, :], k2_s[r, g, b, 0:P], q16_s[r, b, g, :], start=True,
                                  stop=True).then_inc(s_full[n % NS], 1)
                    n = score_no[(*arg, "x", HG)]
                    ps = next_scores(n)
                    for j in range(HG):
                        r = slice(32 * j, 32 * j + 32)
                        ins = pe.matmul(ps[r, :], k2_s[r, g, b, P:CW], q16_s[r, b, g, :], start=True, stop=True)
                    ins.then_inc(s_full[n % NS], 1)
                elif stage == "values2":
                    b, g = arg
                    if group2_no[arg] > 0:
                        pe.wait_ge(o2_moved, group2_no[arg])
                    if g == 0:
                        wait_moved(pe, ("v2a",))
                        wait_moved(pe, ("v2b",))
                    slot = slot2_no[arg]
                    for j in range(HG):
                        n = score_no[(*arg, "x", j)]
                        pe.wait_ge(s_moved[n % NS], n // NS + 1)
                        pe.matmul(obank2[32 * j:32 * j + 32, :], v2a_s[:, b, HG * g + j, :],
                                  prob2_s[:, slot % NP, j, :], start=True, stop=False)
                    n = score_no[(*arg, "x", HG)]
                    pe.wait_ge(s_moved[n % NS], n // NS + 1)
                    for j in range(HG):
                        r = slice(32 * j, 32 * j + NCB)
                        ins = pe.matmul(obank2[32 * j:32 * j + 32, :], v2b_s[r, b, HG * g + j, :],
                                        probb_s[r, slot % 2, :], start=False, stop=True)
                    ins.then_inc(slot2_used, 1)
                elif stage == "joined":
                    b, = arg
                    wait_moved(pe, ("oT", b, G - 1))
                    transposes(("aT", b), lambda t: att_s[:, b, t, :])
                elif stage == "project":
                    b, = arg
                    wait_moved(pe, ("aT", b))
                    ps = take(pe, ("proj", b))
                    for t in range(TT):
                        ins = pe.matmul(ps[:, t * D:(t + 1) * D], xT_s[:, b * L + t * P:b * L + (t + 1) * P], wproj_s[:, :],
                                        start=True, stop=True)
                    ins.then_inc(filled(("proj", b)), 1)
                elif stage == "turn2":
                    b, = arg
                    normed(("x2T", b), b)
                elif stage == "query2":
                    b, = arg
                    wait_moved(pe, ("x2T", b))
                    ps = take(pe, ("q2", b))
                    pe.matmul(ps[:, :], wq_s[:, :], xT_s[:, b * L:(b + 1) * L], start=True,
                              stop=True).then_inc(filled(("q2", b)), 1)
                elif stage == "spread2":
                    b, g = arg
                    r = slice(32 * g, 32 * g + 32)
                    wait_moved(pe, ("q2", b))
                    spread(("sq2", b, g), qhi_s[r, b, :], qlo_s[r, b, :], 0, g)
                elif stage == "turn3":
                    normed(("x3T", arg[0]), arg[0])
                elif stage == "router_hidden":
                    b, m = arg
                    wait_moved(pe, ("x3T", b))
                    pe.wait_ge(in_router, 16 * 3)
                    ps = take(pe, ("r", b, m))
                    pe.matmul(ps[:, :], rw1_s[:, m * P:(m + 1) * P], xT_s[:, b * L:(b + 1) * L], start=True,
                              stop=True).then_inc(filled(("r", b, m)), 1)
                elif stage == "logits":
                    b, = arg
                    ps = take(pe, ("lg", b))
                    for m in range(M):
                        wait_moved(pe, ("r", b, m))
                    for t in range(TT):
                        for m in range(M):
                            ins = pe.matmul(ps[:, t * E:(t + 1) * E], rT_s[:, m, t * P:(t + 1) * P], rw2_s[:, m, :],
                                            start=(m == 0), stop=(m == M - 1))
                    ins.then_inc(filled(("lg", b)), 1)
                elif stage == "places":
                    b, = arg
                    counts["pick"] += 5
                    pe.wait_ge(pick_done, counts["pick"])
                    ps = take(pe, ("pos", b))
                    for t in range(TT):
                        tile = b * TT + t
                        for s in range(tile + 1):
                            ins = pe.matmul(ps[:, t * E:(t + 1) * E], count_s[:, 0 if s == tile else 1, :],
                                            picks_s[:, s, :], start=(s == 0), stop=(s == tile))
                    ins.then_inc(filled(("pos", b)), 1)
                elif stage == "gates":
                    b, = arg
                    counts["gate"] += 6
                    pe.wait_ge(gate_done, counts["gate"])
                    transposes(("gT", b), lambda t: gate_s[:, b * TT + t, :], rows=E)
                elif stage == "bias_out":
                    b, = arg
                    wait_moved(pe, ("gT", b))
                    ps = take(pe, ("b2", b))
                    for t in range(TT):
                        ins = pe.matmul(ps[:, t * D:(t + 1) * D], gateT_s[:, b, t * P:(t + 1) * P], eb2_s[:, :],
                                        start=True, stop=True)
                    ins.then_inc(filled(("b2", b)), 1)
                elif stage == "hidden":
                    b, e, m = arg
                    if m == 0:
                        pe.wait_ge(in_e1[e], 16)
                    ps = take(pe, ("h", b, e, m))
                    pe.matmul(ps[:, :], ew1_s[:, e, m * P:(m + 1) * P], xT_s[:, b * L:(b + 1) * L], start=True,
                              stop=True).then_inc(filled(("h", b, e, m)), 1)
                elif stage == "expert_out":
                    b, e = arg
                    pe.wait_ge(in_e2[e], 16)
                    for m in range(M):
                        wait_moved(pe, ("h", b, e, m))
                    ps = take(pe, ("y", b, e))
                    for t in range(TT):
                        for m in range(M):
                            ins = pe.matmul(ps[:, t * D:(t + 1) * D], hT_s[:, (b * E + e) % 2, m, t * P:(t + 1) * P],
                                            ew2_s[:, e, m, :], start=(m == 0), stop=(m == M - 1))
                    ins.then_inc(filled(("y", b, e)), 1)
                elif stage == "heads1":
                    n = group_no[arg]
                    pe.wait_ge(o_moved, n + 1)
                    transposes(("oT", *arg), lambda t: o_s[:, n % 2, t * P:(t + 1) * P])
                elif stage == "heads2":
                    n = group2_no[arg]
                    pe.wait_ge(o2_moved, n + 1)
                    transposes(("oT2", *arg), lambda t: o2_s[:, n % 2, t * P:(t + 1) * P])


def constants():
    pos = (np.arange(L, dtype=np.float32) * np.float32((1.0 + np.sqrt(5.0)) / 2.0)) % np.float32(1.0)
    bias = np.exp(-np.abs(pos[:, None] - pos[None, :])) + np.float32(1e-8)
    spread = np.zeros((P, 4, P), np.float16)
    for kind, parts in enumerate(((0, 1), (2,), (0, 2), (1,))):
        for j in range(HG):
            for t in parts:
                for d in range(DH):
                    spread[j * DH + d::32, kind, 32 * j + t * DH + d] = 1
    count = np.stack([np.triu(np.ones((P, P), np.float16), 1), np.ones((P, P), np.float16)], 1)
    size = np.zeros((P, 32), np.float16)
    shift = np.zeros((P, 1), np.float32)
    for h in range(H):
        size[h * DH:(h + 1) * DH, h] = 1
    for j in range(HG):
        shift[32 * j + 3 * DH:32 * j + 3 * DH + 2] = -SHIFT
    iota = np.tile(np.arange(E, dtype=np.float32), (P, 1))
    return {
        "bias": np.ascontiguousarray(bias.astype(np.float32).reshape(KC, P, L).transpose(1, 0, 2)),
        "full": np.concatenate([np.eye(P, dtype=np.float32), iota, shift], 1),
        "half": np.concatenate([spread.reshape(P, -1), count.reshape(P, -1), size], 1),
    }


def kernel(x, ctx_768, L0_attn_w_qkv, L0_attn_w_proj, L0_attn_b_proj, L0_xattn_norm_g, L0_xattn_norm_b,
           L0_xattn_tnorm_g, L0_xattn_tnorm_b, L0_xattn_Wq, L0_xattn_bq, L0_xattn_Wk, L0_xattn_bk, L0_xattn_Wv,
           L0_xattn_bv, L0_ffn_rw1, L0_ffn_rb1, L0_ffn_rw2, L0_ffn_rb2, L0_ffn_ew1, L0_ffn_eb1, L0_ffn_ew2,
           L0_ffn_eb2):
    import concourse.bacc as _bacc
    from concourse.bass_utils import run_bass_kernel_spmd as _run

    nc = _bacc.Bacc("TRN2", target_bir_lowering=False, num_devices=1)
    fill = np.zeros(P - CD, np.float32)
    vectors = np.concatenate([np.asarray(v) for v in (
        L0_ffn_eb1.reshape(-1), L0_ffn_rb1, L0_xattn_norm_g, L0_xattn_norm_b, L0_xattn_bq, L0_xattn_bk,
        L0_xattn_tnorm_g, fill, L0_xattn_tnorm_b, fill)]).reshape(VROWS, P)
    rows = np.concatenate([np.asarray(v) for v in (L0_attn_b_proj, L0_xattn_bv, L0_ffn_rb2)])
    wkv = np.concatenate([np.asarray(L0_xattn_Wk), np.asarray(L0_xattn_Wv)], 1)
    given = {"x": x, "ctx_in": ctx_768, "w_qkv": L0_attn_w_qkv, "w_proj": L0_attn_w_proj, "wq": L0_xattn_Wq,
             "rw1": L0_ffn_rw1, "rw2": L0_ffn_rw2, "ew1": L0_ffn_ew1, "ew2": L0_ffn_ew2, "eb2": L0_ffn_eb2,
             "wkv": wkv, "vectors": vectors, "rows": rows}
    given.update({f"c_{k}": v for k, v in constants().items()})
    arrays, args = {}, {}
    for name, a in given.items():
        a = np.ascontiguousarray(a)
        arrays[name] = a
        args[name] = nc.dram_tensor(name, a.shape, mybir.dt.from_np(a.dtype), kind="ExternalInput").ap()
    out = nc.dram_tensor("out", (B, L, D), F32, kind="ExternalOutput").ap()
    build(nc, out=out, **args)
    r = _run(nc, [arrays], core_ids=[0])
    return r.results[0]["out"]
```

```python
from contextlib import ExitStack

import concourse.bass as bass
import numpy as np
from concourse import mybir

F32 = mybir.dt.float32
F16 = mybir.dt.float16
BF16 = mybir.dt.bfloat16
I32 = mybir.dt.int32
U32 = mybir.dt.uint32
ALU = mybir.AluOpType
ACT = mybir.ActivationFunctionType
AX = mybir.AxisListType

P = 128
B = 2
L = 512
D = 128
H = 16
DH = D // H
TT = L // P
NT = B * TT
HG = 4
G = H // HG
KC = L // P
NC = 154
CD = 96
NCB = NC - P
CW = P + 32
E = 8
F = 512
M = F // P
CAP = 512
EPS = 1e-5
SCALE = float(DH) ** -0.5
NB = 3
NS = 3
WARM = 14
LAG = 6
NP1 = 3
NP = 2
BEHIND = 1
LIMIT = 60.0
SHIFT = 64.0
WUP = 64.0
HUP = 4.0
VROWS = 42

START = (
    ("norm1", 0), ("root", 0), ("scale1", 0), ("norm1", 1), ("turn1", 0), ("root", 1), ("qkv", 0),
    ("ctx_norm",), ("ctx_root",), ("spread1", 0, 0), ("scale1", 1), ("spread1", 0, 1), ("sizes", 0),
    ("spread1", 0, 3), ("spread1", 0, 2), ("vectors",), ("flag", 0), ("turn1", 1), ("ctx_scale",),
    ("guard", 0),
)

FILL_0 = (
    0, 1, 0, 1, 0, 1, 0, 1, 0, 2, 0, 2, 0, 0, 0, 1, 0, 2, 0, 0, 0, 1, 0, 2, 0, 1, 0, 4, 0, 1, 1, 0, 0, 0,
)
FILL_1 = (
    1, 1, 1, 1, 0, 1, 1, 1, 0, 0, 0, 0, 1, 1, 0, 1, 0, 0, 0, 1, 1, 0, 1, 0, 2, 0, 0, 1, 0, 1, 0, 1, 0, 1, 1,
    3, 3, 3, 3, 1, 1, 1, 0,
)
FILL_2 = (
    2, 3, 2, 2, 2, 2, 3, 2, 2, 2, 2, 0, 1, 0, 1, 1, 1, 1, 0, 0, 2, 2, 0, 0, 3, 0, 1, 1, 0, 0, 0, 1, 1, 0, 2,
    1, 0, 2, 1, 2, 2, 3, 4,
)
FILL_3 = (
    2, 2, 2, 3, 0, 3, 3, 3, 4,
)


def blend(main, filler, counts):
    out = []
    filler = list(filler)
    for i, step in enumerate(main):
        out.append(step)
        for _ in range(counts[i] if i < len(counts) else 0):
            if filler:
                out.append(filler.pop(0))
    return out, filler


def schedule():

    def attention(b):
        units = [(g, c) for g in range(G) for c in range(KC)]
        out = []
        for i, (g, c) in enumerate(units):
            out.append([("scores1", b, g, c, 0)])
            out.append([("scores1", b, g, c, 1)])
            if i >= BEHIND:
                out[-1].append(("values1", b, *units[i - BEHIND]))
            if c == BEHIND - 1 and g > 0:
                out[-1].append(("out1", b, g - 1))
            if c == BEHIND and g > 0:
                out[-1].append(("heads1", b, g - 1))
            if i % 2 == 0:
                out[-1].append(("round", (b * len(units) + i) // 2))
            elif b * len(units) + i > 1:
                out[-1].append(("remainder", (b * len(units) + i) // 2 - 1))
        if b == B - 1:
            out[-1].append(("remainder", 2 * E - 1))
        out += [[("values1", b, *units[i])] for i in range(len(units) - BEHIND, len(units))]
        return out + [[("out1", b, G - 1)], [("heads1", b, G - 1)]]

    def after_attention(b):
        return [("joined", b), ("project", b), ("norm2", b), ("root", b), ("scale2", b), ("turn2", b),
                ("query2", b), ("sizes", b + B)] + [("spread2", b, g) for g in range(G)] + \
               [("flag", b + B), ("guard", b + B)]

    def cross(b):
        out = []
        for g in range(G + 1):
            if g < G:
                out += [("scores2", b, g, 0), ("scores2", b, g, 1)]
            if g > 0:
                out += [("values2", b, g - 1), ("out2", b, g - 1)]
            if g > 1:
                out.append(("heads2", b, g - 2))
        return out + [("heads2", b, G - 1), ("norm3", b), ("root", b), ("scale3", b), ("turn3", b)]

    def router(b):
        return [("router_hidden", b, m) for m in range(M)] + \
               [("partials", b), ("logits", b), ("places", b), ("gates", b), ("bias_out", b)]

    def experts(b):
        hidden = [("hidden", b, *divmod(k, M)) for k in range(E * M)]
        outs = [("expert_out", b, *divmod(k, TT)) for k in range(E * TT)]
        out = [("split3", b)]
        for k in range(E * M + LAG):
            if k >= LAG:
                out.append(outs[k - LAG])
            if k < E * M:
                out.append(hidden[k])
        return out

    def flat(groups):
        return [s for g in groups for s in g]

    plan = list(START)
    early = [("qkv", 1), ("ctx_turn",), ("sizes", 1), ("ctx_keys",)] + [("ctx_spread", g) for g in range(G)] + \
            [("ctx_values",)] + [("spread1", 1, g) for g in range(G)] + [("flag", 1), ("guard", 1)]
    plan += flat(sum(blend(attention(0), [[s] for s in early], FILL_0), []))
    chain = after_attention(0) + cross(0) + router(0)[0:M]
    plan += flat(sum(blend([[s] for s in chain], attention(1), FILL_1), []))
    steps, left = blend(router(0)[M:] + after_attention(1) + cross(1), experts(0), FILL_2)
    plan += steps
    plan += sum(blend(router(1), left + experts(1), FILL_3), [])
    return plan


BANKS = {
    "vectors": ["vecT"], "turn1": ["xT"], "qkv": ["q", "k", "v"], "spread1": ["sq", "sk"], "sizes": ["size"],
    "flag": ["flag"], "ctx_turn": ["cT"], "ctx_keys": ["k2"], "ctx_spread": ["sk2"],
    "ctx_values": ["v2a", "v2b"],
    "heads1": ["oT"], "joined": ["aT"], "project": ["proj"], "turn2": ["x2T"], "query2": ["q2"], "spread2": ["sq2"],
    "heads2": ["oT2"], "turn3": ["x3T"], "router_hidden": ["r"], "partials": ["lp"], "logits": ["lg"],
    "places": ["pos"], "gates": ["gT"], "bias_out": ["b2"], "hidden": ["h"],
}


def build(nc, x, ctx_in, w_qkv, w_proj, wq, rw1, rw2, ew1, ew2, eb2, wkv, vectors, rows, c_bias, c_full, c_half,
          out):
    plan = schedule()
    use = {}
    for step in plan:
        for name in BANKS.get(step[0], []):
            use[(name, *step[1:])] = len(use)
    score_no = {}
    slot_no = {}
    group_no = {}
    slot2_no = {}
    group2_no = {}
    scores_before = {}
    hi_after = {}
    squares_no = {}

    def pair(half, last=HG):
        return range(HG // 2) if half == 0 else range(HG // 2, last)

    rounded = 0
    normed_tiles = 0
    normed_after = {}
    for step in plan:
        if step[0] in ("scale1", "scale2", "scale3"):
            normed_tiles += TT
            normed_after[({"scale1": "xT", "scale2": "x2T", "scale3": "x3T"}[step[0]], step[1])] = normed_tiles
        if step[0] == "ctx_scale":
            normed_tiles += 4
            normed_after["context"] = normed_tiles
        rounded += {"qkv": 2, "ctx_keys": 1, "query2": 1}.get(step[0], 0)
        if step[0] == "sizes":
            squares_no[step[1]] = len(squares_no)
            hi_after[step[1]] = rounded
        if step[0] == "guard":
            scores_before[step[1]] = len(score_no)
        if step[0] == "scores1":
            slot_no.setdefault(step[1:4], len(slot_no))
            for j in pair(step[4]):
                score_no[(*step[1:4], j)] = len(score_no)
        if step[0] == "scores2":
            slot2_no.setdefault(step[1:3], len(slot2_no))
            for j in pair(step[3], HG + 1):
                score_no[(*step[1:3], "x", j)] = len(score_no)
        if step[0] == "out1":
            group_no[step[1:]] = len(group_no)
        if step[0] == "out2":
            group2_no[step[1:]] = len(group2_no)

    with ExitStack() as stack:
        def sb(name, shape, dt=F32):
            return stack.enter_context(nc.sbuf_tensor(name, shape, dt))

        def sem(name):
            return stack.enter_context(nc.semaphore(name))

        wqkv_s = sb("wqkv_s", [P, 3 * D])
        wproj_s = sb("wproj_s", [P, D])
        wq_s = sb("wq_s", [P, D])
        wkv_s = sb("wkv_s", [CD, 2 * D])
        wk_s, wv_s = wkv_s[:, 0:D], wkv_s[:, D:2 * D]
        rw1_s = sb("rw1_s", [P, F])
        rw2_s = sb("rw2_s", [P, M, 32])
        ew1hi_s = sb("ew1hi_s", [P, E, F], F16)
        ew1lo_s = sb("ew1lo_s", [P, E, F], F16)
        ew2hi_s = sb("ew2hi_s", [P, E, F], F16)
        ew2lo_s = sb("ew2lo_s", [P, E, F], F16)
        eb2_s = sb("eb2_s", [E, D])
        rows_s = sb("rows_s", [P, 2 * D + E])
        bproj_s, bv_s, rb2_s = rows_s[:, 0:D], rows_s[:, D:2 * D], rows_s[:, 2 * D:2 * D + E]
        vec_s = sb("vec_s", [VROWS, P])
        col_s = sb("col_s", [P, VROWS])
        bias_s = sb("bias_s", [P, KC, L])
        full_s = sb("full_s", [P, P + E + 1 + E])
        ident_s, iota_s, shift_s = full_s[:, 0:P], full_s[:, P:P + E], full_s[:, P + E:P + E + 1]
        sum_s = full_s[:, P + E + 1:P + 2 * E + 1]
        half_s = sb("half_s", [P, 6 * P + 32], F16)
        spread_s = half_s[:, 0:4 * P].rearrange("p (k c) -> p k c", k=4)
        count_s = half_s[:, 4 * P:6 * P].rearrange("p (k c) -> p k c", k=2)
        size_s = half_s[:, 6 * P:6 * P + 32]
        ones_s = sb("ones_s", [64, 1])
        x_s = sb("x_s", [P, NT, D])
        xn_s = sb("xn_s", [P, NT, D])
        xT_s = sb("xT_s", [P, B * L])
        stats_s = sb("stats_s", [P, NT + 4, 6])
        mv_s = sb("mv_s", [P, NT + 4, 2])
        rstd_s = sb("rstd_s", [P, NT + 4, 4])
        qhi_s = sb("qhi_s", [P, B, L], F16)
        qlo_s = sb("qlo_s", [P, B, L], F16)
        khi_s = sb("khi_s", [P, B, L], F16)
        klo_s = sb("klo_s", [P, B, L], F16)
        sq_s = sb("sq_s", [P, B, 2, L], BF16)
        size_max_s = sb("size_max_s", [64, 2 * B])
        large_s = sb("large_s", [64, 2 * B])
        flag_s = sb("flag_s", [1, 2 * B], I32)
        max_s = sb("max_s", [P, TT, H])
        maxhi_s = sb("maxhi_s", [H, L], F16)
        maxlo_s = sb("maxlo_s", [H, L], F16)
        q16_s = sb("q16_s", [P, B, G, L], F16)
        k16_s = sb("k16_s", [P, B, G, L], F16)
        kz_s = sb("kz_s", [P, 2, HG, L], F16)
        v_s = sb("v_s", [P, B, KC, H, 32])
        prob_s = sb("prob_s", [P, NP1 - 1, HG, L])
        prob2_s = sb("prob2_s", [P, NP, HG, L])
        probb_s = sb("probb_s", [P, 2, L])
        o_s = sb("o_s", [P, 2, L])
        o2_s = sb("o2_s", [P, 2, L])
        rden_s = sb("rden_s", [P, 2, B * G, TT, HG])
        att_s = xn_s[:, :, :].rearrange("p (b t) d -> p b t d", b=B)
        x1_s = sb("x1_s", [P, NT, D])
        ctx_s = sb("ctx_s", [P, B, 2, CD])
        ctxT_s = sb("ctxT_s", [CD, B, CW])
        ctxT4_s = sb("ctxT4_s", [CD, B, HG, 32])
        k2hi_s = sb("k2hi_s", [P, B, CW], F16)
        k2lo_s = sb("k2lo_s", [P, B, CW], F16)
        k2_s = sb("k2_s", [P, G, B, CW], F16)
        v2a_s = sb("v2a_s", [P, B, H, 32])
        v2b_s = sb("v2b_s", [P, B, H, 32])
        top_s = sb("top_s", [P, NT, 8])
        topi_s = sb("topi_s", [P, NT, 8], U32)
        topf_s = sb("topf_s", [P, NT, 2])
        lg_s = sb("lg_s", [P, NT, E])
        partial_s = sb("partial_s", [P, L])
        pick_s = sb("pick_s", [P, NT, 2, E])
        picks_s = sb("picks_s", [P, NT, E], F16)
        pr_s = sb("pr_s", [P, NT, 4])
        gate_s = sb("gate_s", [P, NT, E])
        gatey_s = sb("gatey_s", [P, NT, E])
        gate2_s = sb("gate2_s", [P, NT, 2, E])
        keep_s = sb("keep_s", [P, NT, E])
        gateT_s = sb("gateT_s", [E, B, L])
        rT_s = prob2_s[:, 0, :, :]
        both_s = sb("both_s", [P, 4, M, L], F16)
        raw_s = both_s[:, 0:4, :, :].rearrange("p s m l -> p (s m l)").bitcast(F32).rearrange("p (s w) -> p s w", w=F)
        prob1_s = [prob_s[:, 0, :, :], prob_s[:, 1, :, :], raw_s[:, 4:8, :]]
        free_s = prob_s[:, :, :, :].rearrange("p s j l -> p (s j) l")
        h_s = free_s[:, 0:2, :]
        x3_s = free_s[:, 2:4, :].rearrange("p s l -> p (s l)").bitcast(F16).rearrange("p (b s l) -> p b s l", b=B, s=2)
        third_s = free_s[:, 4:8, :].rearrange("p s l -> p (s l)").bitcast(F16).rearrange("p (s m l) -> p s m l", s=2, m=M)
        hidden_s = [(both_s[:, 0, :, :], both_s[:, 1, :, :]), (both_s[:, 2, :, :], both_s[:, 3, :, :]),
                    (third_s[:, 0, :, :], third_s[:, 1, :, :])]
        x3hi_s, x3lo_s = x3_s[:, :, 0, :], x3_s[:, :, 1, :]

        bank = [stack.enter_context(nc.psum_tensor(f"bank{i}", [P, 512], F32)) for i in range(NB)]
        sbank = [stack.enter_context(nc.psum_tensor(f"sbank{i}", [P, 512], F32)) for i in range(NS)]
        obank = stack.enter_context(nc.psum_tensor("obank", [P, 512], F32))
        obank2 = stack.enter_context(nc.psum_tensor("obank2", [P, 512], F32))

        in_x = [sem(f"in_x{b}") for b in range(B)]
        warm_zero = sem("warm_zero")
        in_first = sem("in_first")
        in_attn = sem("in_attn")
        in_ctx = sem("in_ctx")
        in_cross = sem("in_cross")
        in_router = sem("in_router")
        in_raw = [sem(f"in_raw{i}") for i in range(4)]
        weights_hi = sem("weights_hi")
        weights_done = sem("weights_done")
        x3_hi = sem("x3_hi")
        x3_split = sem("x3_split")
        h_split = sem("h_split")
        y_full = sem("y_full")
        y_moved = sem("y_moved")
        full = [sem(f"bank_full{i}") for i in range(NB)]
        moved = [sem(f"bank_moved{i}") for i in range(NB)]
        s_full = [sem(f"scores_full{i}") for i in range(NS)]
        s_moved = [sem(f"scores_moved{i}") for i in range(NS)]
        hi_done = sem("hi_done")
        biased = sem("biased")
        biased_by_pool = sem("biased_by_pool")
        slot_used = sem("slot_used")
        slot2_used = sem("slot2_used")
        squared = sem("squared")
        kz_zero = sem("kz_zero")
        kz_ready = [sem(f"kz_ready{i}") for i in range(2)]
        size_done = sem("size_done")
        row_full = [sem(f"row_scores_full{i}") for i in range(2 * B)]
        row_max = [sem(f"row_max_done{i}") for i in range(2 * B)]
        turned = [sem(f"row_max_turned{i}") for i in range(2 * B)]
        halves = [sem(f"row_max_halves{i}") for i in range(2 * B)]
        shifted = [sem(f"row_max_in_place{i}") for i in range(2 * B)]
        o_moved = sem("o_moved")
        o2_moved = sem("o2_moved")
        zeroed = sem("zeroed")
        ones_done = sem("ones_done")
        pads = sem("pads")
        xb_done = sem("xb_done")
        stats_done = sem("stats_done")
        aggr_done = sem("aggr_done")
        rstd_done = sem("rstd_done")
        var_done = sem("var_done")
        root_done = sem("root_done")
        xn_done = sem("xn_done")
        den_done = sem("den_done")
        den2_done = sem("den2_done")
        x2_done = sem("x2_done")
        route_done = sem("route_done")
        exp_done = sem("exp_done")
        pick_done = sem("pick_done")
        gate_done = sem("gate_done")
        stored = sem("stored")

        def bank_of(key):
            return bank[use[key] % NB]

        def take(pe, key):
            n = use[key]
            if n >= NB:
                pe.wait_ge(moved[n % NB], n // NB)
            return bank[n % NB]

        def filled(key):
            return full[use[key] % NB]

        def wait_full(eng, key):
            n = use[key]
            eng.wait_ge(full[n % NB], n // NB + 1)
            return bank[n % NB]

        def emptied(key):
            return moved[use[key] % NB]

        def wait_moved(eng, key):
            n = use[key]
            eng.wait_ge(moved[n % NB], n // NB + 1)

        def bias_pair(eng, arg, half, done):
            slot = slot_no[arg]
            n = score_no[(*arg, 2 * half + 1)]
            eng.wait_ge(s_moved[(n - 1) % NS], (n - 1) // NS + 1)
            eng.wait_ge(s_moved[n % NS], n // NS + 1)
            pr = prob1_s[slot % NP1][:, 2 * half:2 * half + 2, :]
            eng.tensor_tensor(pr, pr, bias_s[:, arg[2]:arg[2] + 1, :].to_broadcast([P, 2, L]), ALU.mult).then_inc(done, 1)

        def y_bank(b, e):
            return obank2 if b == 1 and e % 2 == 1 else obank

        def tiles(b):
            return slice(b * TT, (b + 1) * TT)

        def too_large(eng, call):
            wait_moved(eng, ("flag", call))
            return eng.value_load(flag_s[0:1, call:call + 1], min_val=0, max_val=64)

        def operands(call):
            b = call % B
            if call < B:
                return lambda r, g: q16_s[r, b, g, :], lambda r, g: k16_s[r, b, g, :], L
            return lambda r, g: q16_s[r, b, g, :], lambda r, g: k2_s[r, g, b, 0:NC], NC

        block = stack.enter_context(nc.Block())

        @block.sync
        def _(sp):
            sp.dma_start(x_s[:, 0:TT, :], x[0].rearrange("(t p) d -> p t d", p=P)).then_inc(in_x[0], 16)
            sp.dma_start(wqkv_s[:, :], w_qkv).then_inc(in_first, 16)
            sp.dma_start(half_s[:, :], c_half).then_inc(in_first, 16)
            sp.dma_start(x_s[:, TT:NT, :], x[1].rearrange("(t p) d -> p t d", p=P)).then_inc(in_x[1], 16)
            sp.dma_start(vec_s[:, :], vectors).then_inc(in_ctx, 16)
            sp.dma_start(ctx_s[:, :, 0, :], ctx_in[:, 0:P, :].rearrange("b k c -> k b c")).then_inc(in_ctx, 16)
            sp.dma_start(ctx_s[0:NCB, :, 1, :], ctx_in[:, P:NC, :].rearrange("b k c -> k b c")).then_inc(in_ctx, 16)
            sp.dma_start(rows_s[:, :], rows.partition_broadcast(P)).then_inc(in_cross, 16)
            sp.dma_start(wkv_s[:, :], wkv).then_inc(in_cross, 16)
            sp.dma_start(bias_s[:, :, :], c_bias).then_inc(in_attn, 16)
            sp.dma_start(wproj_s[:, :], w_proj).then_inc(in_cross, 16)
            sp.dma_start(wq_s[:, :], wq).then_inc(in_cross, 16)
            sp.dma_start(rw1_s[:, :], rw1).then_inc(in_router, 16)
            sp.dma_start(eb2_s[:, :], eb2).then_inc(in_router, 16)
            def load_weights(k):
                e, second = divmod(k, 2)
                if k >= 4:
                    sp.wait_ge(weights_done, k - 3)
                if second:
                    sp.dma_start(raw_s[:, k % 4, :].rearrange("p (m c) -> p m c", m=M),
                                 ew2[e].rearrange("(m p) c -> p m c", p=P)).then_inc(in_raw[k % 4], 16)
                else:
                    sp.dma_start(raw_s[:, k % 4, :], ew1[e]).then_inc(in_raw[k % 4], 16)

            for k in range(4):
                load_weights(k)

            def place_keys(n):
                b, g = divmod(n, G)
                wait_moved(sp, ("sk", b, g))
                if n >= 2:
                    last = score_no[(*divmod(n - 2, G), KC - 1, HG - 1)]
                    sp.wait_ge(s_full[last % NS], last // NS + 1)
                for j in range(HG):
                    r = slice(32 * j, 32 * j + 32)
                    sp.dma_start(kz_s[r, n % 2, j, :], k16_s[r, b, g, :]).then_inc(kz_ready[n % 2], 16)

            sp.wait_ge(kz_zero, 2)
            sp.dma_start(rw2_s[:, :, 0:E], rw2.rearrange("(m p) e -> p m e", p=P)).then_inc(in_router, 16)
            for step in plan:
                if step[0] == "spread1" and step[1:] == (0, 0):
                    place_keys(0)
                if step[0] == "scores1" and step[3:] == (0, 0) and step[1:3] != (B - 1, G - 1):
                    place_keys(step[1] * G + step[2] + 1)
                if step[0] == "remainder" and step[1] + 4 < 2 * E:
                    load_weights(step[1] + 4)
                if step[0] == "guard":
                    call = step[1]
                    with sp.If(too_large(sp, call) > 0):
                        sp.wait_ge(halves[call], 2)
                        for part, half in enumerate((maxhi_s, maxlo_s)):
                            for g in range(G):
                                for j in range(HG):
                                    p = 32 * j + 3 * DH + part
                                    sp.dma_start(q16_s[p:p + 1, call % B, g, :],
                                                 half[HG * g + j:HG * g + j + 1, :]).then_inc(shifted[call], 16)
                if step[0] != "expert_out" or step[2:] != (E - 1, TT - 1):
                    continue
                b = step[1]
                sp.wait_ge(y_moved, (b + 1) * E)
                wait_moved(sp, ("b2", b))
                sp.dma_start(out[b].rearrange("(t p) d -> p t d", p=P), x1_s[:, tiles(b), :]).then_inc(stored, 16)
            sp.wait_ge(stored, 16 * B)

        @block.gpsimd
        def _(pool):
            pool.memset(rw2_s[:, :, :], 0.0).then_inc(kz_zero, 1)
            pool.memset(kz_s[:, :, :, :], 0.0).then_inc(kz_zero, 1)
            pool.memset(ones_s[:, :], 1.0).then_inc(ones_done, 1)
            pool.memset(v_s[:, :, :, :, DH:32], 0.0).then_inc(zeroed, 1)
            pool.memset(v2a_s[:, :, :, DH:32], 0.0).then_inc(zeroed, 1)
            pool.memset(v2b_s[:, :, :, DH:32], 0.0).then_inc(zeroed, 1)
            pool.memset(mv_s[:, NT:NT + 4, :], 1.0).then_inc(pads, 1)
            pool.memset(ctxT4_s[:, :, :, :], 0.0).then_inc(pads, 1)
            pool.memset(ctxT_s[:, :, :], 0.0).then_inc(pads, 1)
            pool.memset(k2hi_s[:, :, :], 0.0).then_inc(pads, 1)
            pool.memset(k2lo_s[:, :, :], 0.0).then_inc(pads, 1)
            pool.wait_ge(zeroed, 3)
            pool.memset(v_s[:, :, :, :, DH:DH + 1], 1.0).then_inc(zeroed, 1)
            pool.memset(v2a_s[:, :, :, DH:DH + 1], 1.0).then_inc(zeroed, 1)
            pool.memset(v2b_s[:, :, :, DH:DH + 1], 1.0).then_inc(zeroed, 1)
            pool.wait_ge(in_x[0], 16)
            pool.wait_ge(in_x[1], 16)
            pool.wait_ge(in_cross, 16 * 4)

            def add_bias(b):
                pool.wait_ge(xn_done, normed_after[("xT", b)])
                for t in range(b * TT, (b + 1) * TT):
                    pool.tensor_tensor(x_s[:, t, :], x_s[:, t, :], bproj_s, ALU.add).then_inc(xb_done, 1)

            add_bias(0)
            for step in plan:
                if step[0] == "round":
                    k, = step[1:]
                    pool.wait_ge(in_raw[k % 4], 16 * (k // 4 + 1))
                    pool.tensor_scalar((ew1hi_s, ew2hi_s)[k % 2][:, k // 2, :], raw_s[:, k % 4, :], WUP, None,
                                       ALU.mult).then_inc(weights_hi, 1)
                if step[0] == "scores1" and slot_no[step[1:4]] % 2 == 1 and step[4] == 1:
                    if slot_no[step[1:4]] == 1:
                        pool.wait_ge(in_attn, 16)
                    bias_pair(pool, step[1:4], 1, biased_by_pool)
                if step == ("turn1", 1):
                    add_bias(1)

        @block.scalar
        def _(act):
            act.dma_start(full_s[:, :], c_full).then_inc(in_first, 16)
            act.preload_act_table_set("natural_log_exp_and_others")

            COL = {"eb1": 0, "rb1": E * M, "norm_g": E * M + M, "norm_b": E * M + M + 1,
                   "bq": E * M + M + 2, "bk": E * M + M + 3}

            def column(name, i=0):
                return col_s[:, COL[name] + i:COL[name] + i + 1]

            def move(key, dst, src, func=ACT.Copy, **kw):
                wait_full(act, key)
                act.activation(dst, src, func, **kw).then_inc(emptied(key), 1)

            roots = 0

            def root(ts):
                act.wait_ge(var_done, roots + 1)
                act.activation(rstd_s[:, ts, 1], rstd_s[:, ts, 0], ACT.Ln).then_inc(root_done, 1)
                act.wait_ge(root_done, 2 * roots + 1)
                act.activation(rstd_s[:, ts, 2], rstd_s[:, ts, 1], ACT.Exp, scale=-0.5).then_inc(root_done, 1)
                return roots + 1

            for step in plan:
                stage, arg = step[0], step[1:]
                if stage == "root":
                    roots = root(tiles(*arg))
                elif stage == "sizes":
                    call, = arg
                    b = call % B
                    act.wait_ge(hi_done, hi_after[call])
                    act.activation(sq_s[:, b, 0, :], qhi_s[:, b, :], ACT.Square).then_inc(squared, 1)
                    k, n = (khi_s[:, b, :], L) if call < B else (k2hi_s[:, b, 0:NC], NC)
                    act.activation(sq_s[:, b, 1, 0:n], k, ACT.Square).then_inc(squared, 1)
                elif stage == "ctx_root":
                    roots = root(slice(NT, NT + 4))
                if stage == "vectors":
                    ps = wait_full(act, ("vecT",))
                    act.activation(col_s[:, 0:E * M], ps[:, 0:E * M], ACT.Copy, scale=HUP)
                    act.activation(col_s[:, E * M:VROWS], ps[:, E * M:VROWS], ACT.Copy).then_inc(emptied(("vecT",)), 1)
                elif stage == "turn1":
                    b, = arg
                    move(("xT", b), xT_s[:, b * L:(b + 1) * L], bank_of(("xT", b))[:, :])
                elif stage == "qkv":
                    b, = arg
                    for key, hi in (("q", qhi_s), ("k", khi_s)):
                        ps = wait_full(act, (key, b))
                        act.activation(hi[:, b, :], ps[:, :], ACT.Copy).then_inc(hi_done, 1)
                    ps = bank_of(("v", b))
                    act.wait_ge(zeroed, 4)
                    move(("v", b), v_s[:, b, :, :, 0:DH], ps[:, :].rearrange("p (c h d) -> p c h d", c=KC, h=H))
                elif stage == "spread1":
                    b, g = arg
                    move(("sq", b, g), q16_s[:, b, g, :], bank_of(("sq", b, g))[:, :])
                elif stage == "ctx_keys":
                    ps = wait_full(act, ("k2",))
                    act.wait_ge(pads, 5)
                    wait_moved(act, ("vecT",))
                    act.activation(k2hi_s[:, :, 0:NC], ps[:, 0:B * CW].rearrange("p (b k) -> p b k", b=B)[:, :, 0:NC],
                                   ACT.Identity, bias=column("bk")).then_inc(hi_done, 1)
                elif stage == "ctx_spread":
                    g, = arg
                    act.wait_ge(in_first, 16 * 3)
                    move(("sk2", g), k2_s[:, g, :, :],
                         bank_of(("sk2", g))[:, 0:B * CW].rearrange("p (b k) -> p b k", b=B),
                         ACT.Identity, bias=shift_s[:, 0:1])
                elif stage == "scores1":
                    *key, half = arg
                    slot = slot_no[tuple(key)]
                    if slot >= NP1 and half == 0:
                        act.wait_ge(slot_used, slot - NP1 + 1)
                    for j in pair(half):
                        n = score_no[(*key, j)]
                        act.wait_ge(s_full[n % NS], n // NS + 1)
                        act.activation(prob1_s[slot % NP1][:, j, :], sbank[n % NS][:, :], ACT.Exp,
                                       scale=SCALE).then_inc(s_moved[n % NS], 1)
                elif stage == "scores2":
                    b, g, half = arg
                    slot = slot2_no[(b, g)]
                    if b > 0 and g == 0 and half == 0:
                        wait_full(act, ("lp", b - 1))
                    if slot >= NP and half == 0:
                        act.wait_ge(slot2_used, slot - NP + 1)
                    for j in pair(half, HG + 1):
                        n = score_no[(b, g, "x", j)]
                        act.wait_ge(s_full[n % NS], n // NS + 1)
                        dst = prob2_s[:, slot % NP, j, :] if j < HG else probb_s[:, slot % 2, :]
                        act.activation(dst, sbank[n % NS][:, :], ACT.Exp,
                                       scale=SCALE).then_inc(s_moved[n % NS], 1)
                elif stage == "out1":
                    b, g = arg
                    n = group_no[arg]
                    act.wait_ge(slot_used, slot_no[(b, g, KC - 1)] + 1)
                    if n >= 2:
                        wait_full(act, ("oT", *divmod(n - 2, G)))
                    act.activation(o_s[:, n % 2, :], obank[:, :], ACT.Copy).then_inc(o_moved, 1)
                elif stage == "out2":
                    n = group2_no[arg]
                    act.wait_ge(slot2_used, slot2_no[arg] + 1)
                    if n >= 2:
                        wait_full(act, ("oT2", *divmod(n - 2, G)))
                    act.activation(o2_s[:, n % 2, :], obank2[:, :], ACT.Copy).then_inc(o2_moved, 1)
                elif stage == "joined":
                    b, = arg
                    move(("aT", b), xT_s[:, b * L:(b + 1) * L], bank_of(("aT", b))[:, :])
                elif stage == "query2":
                    b, = arg
                    ps = wait_full(act, ("q2", b))
                    act.activation(qhi_s[:, b, :], ps[:, :], ACT.Identity, bias=column("bq")).then_inc(hi_done, 1)
                elif stage == "spread2":
                    b, g = arg
                    move(("sq2", b, g), q16_s[:, b, g, :], bank_of(("sq2", b, g))[:, :])
                elif stage == "turn3":
                    b, = arg
                    move(("x3T", b), xT_s[:, b * L:(b + 1) * L], bank_of(("x3T", b))[:, :])
                elif stage == "router_hidden":
                    b, m = arg
                    move(("r", b, m), rT_s[:, m, :], bank_of(("r", b, m))[:, :], ACT.Relu, bias=column("rb1", m))
                elif stage == "partials":
                    b, = arg
                    if b > 0:
                        wait_full(act, ("lg", b - 1))
                    move(("lp", b), partial_s[:, :], bank_of(("lp", b))[:, :])
                elif stage == "places":
                    b, = arg
                    act.wait_ge(route_done, b + 1)
                    act.activation(pr_s[:, tiles(b), 1], pr_s[:, tiles(b), 0], ACT.Exp).then_inc(exp_done, 1)
                elif stage == "gates":
                    b, = arg
                    move(("gT", b), gateT_s[:, b, :], bank_of(("gT", b))[0:E, :])
                elif stage == "split3":
                    b, = arg
                    wait_moved(act, ("x3T", b))
                    act.wait_ge(slot_used, B * G * KC)
                    act.activation(x3hi_s[:, b, :], xT_s[:, b * L:(b + 1) * L], ACT.Copy).then_inc(x3_hi, 1)
                elif stage == "hidden":
                    b, e, m = arg
                    i = b * E + e
                    if m == 0:
                        if i < 2:
                            act.wait_ge(weights_done, 2 * E)
                        elif i >= 3:
                            act.wait_ge(y_full, i - 2)
                    k = i * M + m
                    if k >= 2:
                        act.wait_ge(h_split, k - 1)
                    ps = wait_full(act, ("h", b, e, m))
                    kw = dict(bias=column("eb1", e * M + m), scale=HUP / WUP)
                    act.activation(hidden_s[i % 3][0][:, m, :], ps[:, :], ACT.Relu, **kw)
                    act.activation(h_s[:, k % 2, :], ps[:, :], ACT.Relu, **kw).then_inc(emptied(("h", b, e, m)), 1)

        @block.vector
        def _(dve):
            dve.memset(q16_s[:, 1, 0, :], 0.0).then_inc(warm_zero, 1)
            counts = {"stats": 0, "aggr": 0, "rstd": 0, "root": 0, "hi": 0, "pick": 0, "gate": 0}

            def mean_var(src, rows, where):
                for i, s in enumerate(src):
                    dve.bn_stats(stats_s[0:rows[i], where + i, :], s).then_inc(stats_done, 1)
                counts["stats"] += len(src)
                dve.wait_ge(stats_done, counts["stats"])
                for i in range(len(src)):
                    dve.bn_aggr(mv_s[0:rows[i], where + i, :], stats_s[0:rows[i], where + i, :]).then_inc(aggr_done, 1)
                counts["aggr"] += len(src)
                dve.wait_ge(aggr_done, counts["aggr"])

            def step_rstd(ins):
                ins.then_inc(rstd_done, 1)
                counts["rstd"] += 1
                dve.wait_ge(rstd_done, counts["rstd"])

            def variance(ts, mul, add):
                dve.tensor_scalar(rstd_s[:, ts, 0], mv_s[:, ts, 1], mul, add, ALU.mult, ALU.add).then_inc(var_done, 1)

            def refine(ts):
                counts["root"] += 1
                dve.wait_ge(root_done, 2 * counts["root"])
                r = rstd_s[:, ts, 2]
                step_rstd(dve.tensor_tensor(rstd_s[:, ts, 1], r, r, ALU.mult))
                step_rstd(dve.scalar_tensor_tensor(out=rstd_s[:, ts, 3], in0=rstd_s[:, ts, 1], scalar=-0.5,
                                                   in1=rstd_s[:, ts, 0], op0=ALU.mult, op1=ALU.mult))
                step_rstd(dve.scalar_tensor_tensor(out=r, in0=rstd_s[:, ts, 3], scalar=1.5, in1=r,
                                                   op0=ALU.add, op1=ALU.mult))

            def measure(b, src, mul=1.0, add=EPS):
                ts = tiles(b)
                mean_var([src[:, t, :] for t in range(ts.start, ts.stop)], [P] * TT, ts.start)
                variance(ts, mul, add)

            def normalise(b, src):
                ts = tiles(b)
                refine(ts)
                for t in range(ts.start, ts.stop):
                    dve.tensor_scalar(xn_s[:, t, :], src[:, t, :], mv_s[:, t, 0:1], rstd_s[:, t, 2:3],
                                      ALU.subtract, ALU.mult).then_inc(xn_done, 1)

            def heads(key, kind, den, n, b, g):
                ps = wait_full(dve, (key, b, g))[:, :].rearrange("p (t j r) -> p t j r", t=TT, j=HG)
                dve.reciprocal(rden_s[:, kind, n, :, :], ps[:, :, :, DH]).then_inc(den, 1)
                dve.wait_ge(den, n + 1)
                dst = att_s[:, b, :, g * 32:(g + 1) * 32].rearrange("p t (j d) -> p t j d", j=HG)
                dve.tensor_tensor(dst, ps[:, :, :, 0:DH], rden_s[:, kind, n, :, :].unsqueeze(3).to_broadcast([P, TT, HG, DH]),
                                  ALU.mult).then_inc(emptied((key, b, g)), 1)

            added = None

            def wait_added():
                if added and added[0] == "b2":
                    wait_moved(dve, added)
                elif added:
                    dve.wait_ge(y_moved, added[1] * E + added[2] + 1)

            def pick_step(ins):
                ins.then_inc(pick_done, 1)
                counts["pick"] += 1
                dve.wait_ge(pick_done, counts["pick"])

            def gate_step(ins):
                ins.then_inc(gate_done, 1)
                counts["gate"] += 1
                dve.wait_ge(gate_done, counts["gate"])

            for step in plan:
                stage, arg = step[0], step[1:]
                if stage == "norm1":
                    b, = arg
                    dve.wait_ge(in_x[b], 16)
                    measure(b, x_s)
                elif stage == "scale1":
                    normalise(*arg, x_s)
                elif stage == "qkv":
                    b, = arg
                    for key, hi, lo in (("q", qhi_s, qlo_s), ("k", khi_s, klo_s)):
                        counts["hi"] += 1
                        dve.wait_ge(hi_done, counts["hi"])
                        dve.tensor_tensor(lo[:, b, :], bank_of((key, b))[:, :], hi[:, b, :],
                                          ALU.subtract).then_inc(emptied((key, b)), 1)
                elif stage == "spread1":
                    b, g = arg
                    ps = wait_full(dve, ("sk", b, g))
                    dve.tensor_scalar(k16_s[:, b, g, :], ps[:, :], shift_s[:, 0:1], None,
                                      ALU.add).then_inc(emptied(("sk", b, g)), 1)
                elif stage == "sizes":
                    call, = arg
                    ps = wait_full(dve, ("size", call))
                    if call < B:
                        dve.tensor_reduce(size_max_s[:, call:call + 1], ps[0:64, :], AX.X, ALU.max).then_inc(size_done, 1)
                    else:
                        dve.tensor_reduce(size_max_s[0:32, call:call + 1], ps[0:32, :], AX.X, ALU.max)
                        dve.tensor_reduce(size_max_s[32:64, call:call + 1], ps[32:64, 0:NC], AX.X,
                                          ALU.max).then_inc(size_done, 1)
                    dve.wait_ge(size_done, squares_no[call] + 1)
                    dve.tensor_scalar(large_s[:, call:call + 1], size_max_s[:, call:call + 1], LIMIT / SCALE, None,
                                      ALU.is_gt).then_inc(emptied(("size", call)), 1)
                elif stage == "flag":
                    call, = arg
                    ps = wait_full(dve, ("flag", call))
                    dve.tensor_copy(flag_s[0:1, call:call + 1], ps[0:1, 0:1]).then_inc(emptied(("flag", call)), 1)
                elif stage == "guard":
                    call, = arg
                    n = operands(call)[2]
                    with dve.If(too_large(dve, call) > 0):
                        for i in range(H * TT):
                            h, t = divmod(i, TT)
                            dve.wait_ge(row_full[call], i + 1)
                            dve.tensor_reduce(max_s[:, t, h:h + 1], sbank[i % 2][:, 0:n], AX.X,
                                              ALU.max).then_inc(row_max[call], 1)
                        dve.wait_ge(turned[call], 1)
                        dve.tensor_scalar(maxhi_s[:, :], sbank[2][0:H, :], 1.0 / SHIFT, None,
                                          ALU.mult).then_inc(halves[call], 1)
                        dve.wait_ge(halves[call], 1)
                        dve.scalar_tensor_tensor(out=maxlo_s[:, :], in0=sbank[2][0:H, :], scalar=1.0 / SHIFT,
                                                 in1=maxhi_s[:, :], op0=ALU.mult,
                                                 op1=ALU.subtract).then_inc(halves[call], 1)
                elif stage == "ctx_norm":
                    dve.wait_ge(in_ctx, 16 * 3)
                    rows = [P, NCB, P, NCB]
                    src = [ctx_s[0:rows[i], i // 2, i % 2, :] for i in range(4)]
                    dve.wait_ge(pads, 1)
                    mean_var(src, rows, NT)
                    variance(slice(NT, NT + 4), 1.0, EPS)
                elif stage == "ctx_scale":
                    refine(slice(NT, NT + 4))
                    for i in range(4):
                        r = rows[i]
                        dve.tensor_scalar(src[i], src[i], mv_s[0:r, NT + i, 0:1], rstd_s[0:r, NT + i, 2:3],
                                          ALU.subtract, ALU.mult).then_inc(xn_done, 1)
                elif stage == "ctx_turn":
                    ps = wait_full(dve, ("cT",))[0:CD, 0:B * CW].rearrange("p (b k) -> p b k", b=B)
                    dve.wait_ge(pads, 3)
                    wait_moved(dve, ("vecT",))
                    tg = E * M + M + 4
                    counts["rstd"] += 1
                    dve.tensor_scalar(ctxT_s[:, :, 0:NC], ps[:, :, 0:NC], col_s[0:CD, tg:tg + 1],
                                      col_s[0:CD, tg + 1:tg + 2], ALU.mult, ALU.add).then_inc(rstd_done, 1)
                    dve.wait_ge(rstd_done, counts["rstd"])
                    for b in range(B):
                        ins = dve.tensor_copy(ctxT4_s[:, b, :, 0:NCB],
                                              ctxT_s[:, b:b + 1, P:NC].to_broadcast([CD, HG, NCB]))
                    ins.then_inc(emptied(("cT",)), 1)
                elif stage == "ctx_keys":
                    counts["hi"] += 1
                    dve.wait_ge(hi_done, counts["hi"])
                    bkc = E * M + M + 3
                    ps = bank_of(("k2",))[:, 0:B * CW].rearrange("p (b k) -> p b k", b=B)[:, :, 0:NC]
                    dve.scalar_tensor_tensor(out=k2lo_s[:, :, 0:NC], in0=ps, scalar=col_s[:, bkc:bkc + 1],
                                             in1=k2hi_s[:, :, 0:NC], op0=ALU.add,
                                             op1=ALU.subtract).then_inc(emptied(("k2",)), 1)
                elif stage == "ctx_values":
                    dve.wait_ge(zeroed, 6)
                    dve.wait_ge(in_cross, 16 * 4)
                    for key, dst in (("v2a", v2a_s), ("v2b", v2b_s)):
                        ps = wait_full(dve, (key,))
                        for b in range(B):
                            ins = dve.tensor_tensor(dst[:, b, :, 0:DH],
                                                    ps[:, b * D:(b + 1) * D].rearrange("p (h d) -> p h d", h=H),
                                                    bv_s.rearrange("p (h d) -> p h d", h=H), ALU.add)
                        ins.then_inc(emptied((key,)), 1)
                elif stage == "scores1":
                    slot, half = slot_no[arg[0:3]], arg[3]
                    if slot == 0 and half == 0:
                        dve.wait_ge(in_attn, 16)
                    if slot % 2 == 0 or half == 0:
                        bias_pair(dve, arg[0:3], half, biased)
                elif stage == "remainder":
                    k, = arg
                    hi, lo = ((ew1hi_s, ew1lo_s), (ew2hi_s, ew2lo_s))[k % 2]
                    dve.wait_ge(weights_hi, k + 1)
                    dve.scalar_tensor_tensor(out=lo[:, k // 2, :], in0=raw_s[:, k % 4, :], scalar=WUP,
                                             in1=hi[:, k // 2, :], op0=ALU.mult,
                                             op1=ALU.subtract).then_inc(weights_done, 1)
                elif stage == "heads1":
                    b, g = arg
                    heads("oT", 0, den_done, group_no[arg], b, g)
                elif stage == "heads2":
                    b, g = arg
                    heads("oT2", 1, den2_done, group2_no[arg], b, g)
                    if g == G - 1:
                        wait_moved(dve, ("oT2", b, g))
                        dve.tensor_tensor(x1_s[:, tiles(b), :], x1_s[:, tiles(b), :], att_s[:, b, :, :],
                                          ALU.add).then_inc(x2_done, 1)
                elif stage == "project":
                    b, = arg
                    ps = wait_full(dve, ("proj", b))
                    dve.wait_ge(xb_done, (b + 1) * TT)
                    dve.tensor_tensor(x1_s[:, tiles(b), :], ps[:, :].rearrange("p (t d) -> p t d", t=TT),
                                      x_s[:, tiles(b), :], ALU.add).then_inc(emptied(("proj", b)), 1)
                elif stage == "norm2":
                    b, = arg
                    wait_moved(dve, ("proj", b))
                    measure(b, x1_s, 1.0 + EPS, EPS * EPS)
                elif stage in ("scale2", "scale3"):
                    normalise(*arg, x1_s)
                elif stage == "turn2":
                    b, = arg
                    ps = wait_full(dve, ("x2T", b))
                    gc = E * M + M
                    dve.tensor_scalar(xT_s[:, b * L:(b + 1) * L], ps[:, :], col_s[:, gc:gc + 1], col_s[:, gc + 1:gc + 2],
                                      ALU.mult, ALU.add).then_inc(emptied(("x2T", b)), 1)
                elif stage == "query2":
                    b, = arg
                    gc = E * M + M
                    counts["hi"] += 1
                    dve.wait_ge(hi_done, counts["hi"])
                    dve.scalar_tensor_tensor(out=qlo_s[:, b, :], in0=bank_of(("q2", b))[:, :],
                                             scalar=col_s[:, gc + 2:gc + 3], in1=qhi_s[:, b, :], op0=ALU.add,
                                             op1=ALU.subtract).then_inc(emptied(("q2", b)), 1)
                elif stage == "norm3":
                    b, = arg
                    dve.wait_ge(x2_done, b + 1)
                    measure(b, x1_s)
                elif stage == "logits":
                    b, = arg
                    ts = tiles(b)
                    ps = wait_full(dve, ("lg", b))
                    dve.tensor_tensor(lg_s[:, ts, :], ps[:, 0:TT * E].rearrange("p (t e) -> p t e", t=TT),
                                      rb2_s.unsqueeze(1).to_broadcast([P, TT, E]), ALU.add).then_inc(emptied(("lg", b)), 1)
                    wait_moved(dve, ("lg", b))
                    for t in range(ts.start, ts.stop):
                        ins = dve.max(top_s[:, t, :], lg_s[:, t, :])
                    pick_step(ins)
                    for t in range(ts.start, ts.stop):
                        ins = dve.max_index(topi_s[:, t, :], top_s[:, t, :], lg_s[:, t, :])
                    pick_step(ins)
                    dve.tensor_tensor(pr_s[:, ts, 0], top_s[:, ts, 1], top_s[:, ts, 0],
                                      ALU.subtract).then_inc(route_done, 1)
                    pick_step(dve.tensor_copy(topf_s[:, ts, :], topi_s[:, ts, 0:2]))
                    for k in range(2):
                        ins = dve.tensor_tensor(pick_s[:, ts, k, :], iota_s.unsqueeze(1).to_broadcast([P, TT, E]),
                                                topf_s[:, ts, k:k + 1].to_broadcast([P, TT, E]), ALU.is_equal)
                    pick_step(ins)
                    pick_step(dve.tensor_tensor(picks_s[:, ts, :], pick_s[:, ts, 0, :], pick_s[:, ts, 1, :], ALU.add))
                elif stage == "places":
                    b, = arg
                    ts = tiles(b)
                    dve.wait_ge(exp_done, b + 1)
                    gate_step(dve.tensor_scalar(pr_s[:, ts, 2], pr_s[:, ts, 1], 1.0, None, ALU.add))
                    gate_step(dve.reciprocal(pr_s[:, ts, 3], pr_s[:, ts, 2]))
                    gate_step(dve.tensor_tensor(pr_s[:, ts, 2], pr_s[:, ts, 1], pr_s[:, ts, 3], ALU.mult))
                    for k in range(2):
                        ins = dve.tensor_tensor(gate2_s[:, ts, k, :], pick_s[:, ts, k, :],
                                                pr_s[:, ts, 3 - k:4 - k].to_broadcast([P, TT, E]), ALU.mult)
                    gate_step(ins)
                    gate_step(dve.tensor_tensor(gate2_s[:, ts, 0, :], gate2_s[:, ts, 0, :], gate2_s[:, ts, 1, :], ALU.add))
                    ps = wait_full(dve, ("pos", b))
                    dve.tensor_scalar(keep_s[:, ts, :], ps[:, 0:TT * E].rearrange("p (t e) -> p t e", t=TT), float(CAP),
                                      None, ALU.is_lt).then_inc(emptied(("pos", b)), 1)
                    wait_moved(dve, ("pos", b))
                    dve.scalar_tensor_tensor(out=gatey_s[:, ts, :], in0=gate2_s[:, ts, 0, :], scalar=1.0 / (WUP * HUP),
                                             in1=keep_s[:, ts, :], op0=ALU.mult, op1=ALU.mult)
                    gate_step(dve.tensor_tensor(gate_s[:, ts, :], gate2_s[:, ts, 0, :], keep_s[:, ts, :], ALU.mult))
                elif stage == "bias_out":
                    b, = arg
                    ps = wait_full(dve, ("b2", b))
                    wait_added()
                    added = ("b2", b)
                    dve.tensor_tensor(x1_s[:, tiles(b), :], ps[:, :].rearrange("p (t d) -> p t d", t=TT),
                                      x1_s[:, tiles(b), :], ALU.add).then_inc(emptied(("b2", b)), 1)
                elif stage == "split3":
                    b, = arg
                    dve.wait_ge(x3_hi, b + 1)
                    dve.tensor_tensor(x3lo_s[:, b, :], xT_s[:, b * L:(b + 1) * L], x3hi_s[:, b, :],
                                      ALU.subtract).then_inc(x3_split, 1)
                elif stage == "hidden":
                    b, e, m = arg
                    i = b * E + e
                    wait_moved(dve, ("h", b, e, m))
                    hi, lo = hidden_s[i % 3]
                    dve.tensor_tensor(lo[:, m, :], h_s[:, (i * M + m) % 2, :], hi[:, m, :],
                                      ALU.subtract).then_inc(h_split, 1)
                elif stage == "expert_out" and arg[2] == TT - 1:
                    b, e, t = arg
                    wait_added()
                    added = ("y", b, e)
                    dve.wait_ge(y_full, b * E + e + 1)
                    ps = y_bank(b, e)
                    for t in range(TT):
                        ins = dve.scalar_tensor_tensor(out=x1_s[:, b * TT + t, :], in0=ps[:, t * D:(t + 1) * D],
                                                       scalar=gatey_s[:, b * TT + t, e:e + 1],
                                                       in1=x1_s[:, b * TT + t, :], op0=ALU.mult, op1=ALU.add)
                    ins.then_inc(y_moved, 1)

        @block.tensor
        def _(pe):
            counts = {"xn": 0, "gate": 0, "pick": 0}

            pe.wait_ge(warm_zero, 1)
            for _ in range(WARM):
                pe.matmul(sbank[0][:, :], q16_s[:, 1, 0, 0:P], q16_s[:, 1, 0, :], start=True, stop=True)

            def transposes(key, src, n=TT, rows=P):
                ps = take(pe, key)
                for t in range(n):
                    ins = pe.transpose(ps[0:rows, t * P:(t + 1) * P], src(t), ident_s)
                ins.then_inc(filled(key), 1)

            def normed(key, b):
                pe.wait_ge(xn_done, normed_after[key])
                transposes(key, lambda t: xn_s[:, b * TT + t, :])

            def spread(key, hi, lo, side, g):
                ps = take(pe, key)
                r = slice(32 * g, 32 * g + 32)
                n = hi.free_size()
                pe.matmul(ps[:, 0:n], spread_s[r, 2 * side, :], hi, start=True, stop=False)
                pe.matmul(ps[:, 0:n], spread_s[r, 2 * side + 1, :], lo, start=False, stop=True).then_inc(filled(key), 1)

            def next_scores(n):
                if n >= NS:
                    pe.wait_ge(s_moved[n % NS], n // NS)
                return sbank[n % NS]

            for step in plan:
                stage, arg = step[0], step[1:]
                if stage == "vectors":
                    pe.wait_ge(in_ctx, 16 * 3)
                    ps = take(pe, ("vecT",))
                    n = VROWS
                    pe.transpose(ps[:, 0:n], vec_s[0:n, :], ident_s[0:n, 0:n]).then_inc(filled(("vecT",)), 1)
                elif stage == "turn1":
                    if arg[0] == 0:
                        pe.wait_ge(in_first, 16 * 3)
                    normed(("xT", arg[0]), arg[0])
                elif stage == "qkv":
                    b, = arg
                    wait_moved(pe, ("xT", b))
                    for i, key in enumerate(("q", "k")):
                        ps = take(pe, (key, b))
                        pe.matmul(ps[:, :], wqkv_s[:, i * D:(i + 1) * D], xT_s[:, b * L:(b + 1) * L],
                                  start=True, stop=True).then_inc(filled((key, b)), 1)
                    ps = take(pe, ("v", b))
                    for t in range(TT):
                        ins = pe.matmul(ps[:, t * D:(t + 1) * D], xT_s[:, b * L + t * P:b * L + (t + 1) * P],
                                        wqkv_s[:, 2 * D:3 * D], start=True, stop=True)
                    ins.then_inc(filled(("v", b)), 1)
                elif stage == "spread1":
                    b, g = arg
                    r = slice(32 * g, 32 * g + 32)
                    wait_moved(pe, ("q", b))
                    spread(("sq", b, g), qhi_s[r, b, :], qlo_s[r, b, :], 0, g)
                    wait_moved(pe, ("k", b))
                    spread(("sk", b, g), khi_s[r, b, :], klo_s[r, b, :], 1, g)
                elif stage == "sizes":
                    call, = arg
                    n = L if call < B else NC
                    pe.wait_ge(squared, 2 * squares_no[call] + 2)
                    ps = take(pe, ("size", call))
                    pe.matmul(ps[0:32, :], size_s, sq_s[:, call % B, 0, :], start=True, stop=True)
                    pe.matmul(ps[32:64, 0:n], size_s, sq_s[:, call % B, 1, 0:n], start=True,
                              stop=True).then_inc(filled(("size", call)), 1)
                elif stage == "flag":
                    call, = arg
                    wait_moved(pe, ("size", call))
                    pe.wait_ge(ones_done, 1)
                    ps = take(pe, ("flag", call))
                    pe.matmul(ps[0:1, 0:1], large_s[:, call:call + 1], ones_s[:, :], start=True,
                              stop=True).then_inc(filled(("flag", call)), 1)
                elif stage == "guard":
                    call, = arg
                    queries, keys, n = operands(call)
                    with pe.If(too_large(pe, call) > 0):
                        for s in range(NS):
                            used = (scores_before[call] - s + NS - 1) // NS
                            if used > 0:
                                pe.wait_ge(s_moved[s], used)
                        for g in range(G):
                            wait_moved(pe, (("sq" if call < B else "sq2"), call % B, g))
                            wait_moved(pe, ("sk", call % B, g) if call < B else ("sk2", g))
                        for i in range(H * TT):
                            h, t = divmod(i, TT)
                            r = slice(32 * (h % HG), 32 * (h % HG) + 32)
                            if i >= 2:
                                pe.wait_ge(row_max[call], i - 1)
                            pe.matmul(sbank[i % 2][:, 0:n], queries(r, h // HG)[:, t * P:(t + 1) * P],
                                      keys(r, h // HG), start=True, stop=True).then_inc(row_full[call], 1)
                        pe.wait_ge(row_max[call], H * TT)
                        for t in range(TT):
                            ins = pe.transpose(sbank[2][0:H, t * P:(t + 1) * P], max_s[:, t, :], ident_s)
                        ins.then_inc(turned[call], 1)
                        pe.wait_ge(shifted[call], 16 * 2 * H)
                elif stage == "ctx_turn":
                    pe.wait_ge(xn_done, normed_after["context"])
                    ps = take(pe, ("cT",))
                    for b in range(B):
                        pe.transpose(ps[0:CD, b * CW:b * CW + P], ctx_s[:, b, 0, :], ident_s)
                        ins = pe.transpose(ps[0:CD, b * CW + P:b * CW + NC], ctx_s[0:NCB, b, 1, :],
                                           ident_s[0:NCB, 0:NCB])
                    ins.then_inc(filled(("cT",)), 1)
                elif stage == "ctx_keys":
                    wait_moved(pe, ("cT",))
                    pe.wait_ge(in_cross, 16 * 4)
                    ps = take(pe, ("k2",))
                    pe.matmul(ps[:, 0:B * CW], wk_s, ctxT_s[:, :, :], start=True, stop=True).then_inc(filled(("k2",)), 1)
                elif stage == "ctx_spread":
                    g, = arg
                    r = slice(32 * g, 32 * g + 32)
                    wait_moved(pe, ("k2",))
                    spread(("sk2", g), k2hi_s[r, :, :], k2lo_s[r, :, :], 1, g)
                elif stage == "ctx_values":
                    for key, src in (("v2a", lambda b: ctxT_s[:, b, 0:P]), ("v2b", lambda b: ctxT4_s[:, b, :, :])):
                        ps = take(pe, (key,))
                        for b in range(B):
                            ins = pe.matmul(ps[:, b * D:(b + 1) * D], src(b), wv_s, start=True, stop=True)
                        ins.then_inc(filled((key,)), 1)
                elif stage == "scores1":
                    b, g, c, half = arg
                    wait_moved(pe, ("sq", b, g))
                    pe.wait_ge(kz_ready[g % 2], 16 * HG * ((b * G + g) // 2 + 1))
                    for j in pair(half):
                        n = score_no[(b, g, c, j)]
                        ps = next_scores(n)
                        pe.matmul(ps[:, :], kz_s[:, (b * G + g) % 2, j, c * P:(c + 1) * P], q16_s[:, b, g, :],
                                  start=True, stop=True).then_inc(s_full[n % NS], 1)
                elif stage == "values1":
                    b, g, c = arg
                    if c == 0:
                        wait_moved(pe, ("v", b))
                        n = group_no[(b, g)]
                        if n > 0:
                            pe.wait_ge(o_moved, n)
                    slot = slot_no[arg]
                    for j in range(HG):
                        if j == 2 and slot % 2 == 1:
                            pe.wait_ge(biased_by_pool, slot // 2 + 1)
                        elif j % 2 == 0:
                            pe.wait_ge(biased, slot // 2 * 3 + slot % 2 * 2 + j // 2 + 1)
                        ins = pe.matmul(obank[32 * j:32 * j + 32, :], v_s[:, b, c, HG * g + j, :],
                                        prob1_s[slot % NP1][:, j, :], start=(c == 0), stop=(c == KC - 1))
                    ins.then_inc(slot_used, 1)
                elif stage == "scores2":
                    b, g, half = arg
                    wait_moved(pe, ("sq2", b, g))
                    for j in pair(half):
                        n = score_no[(b, g, "x", j)]
                        r = slice(32 * j, 32 * j + 32)
                        ps = next_scores(n)
                        pe.matmul(ps[:, :], k2_s[r, g, b, 0:P], q16_s[r, b, g, :], start=True,
                                  stop=True).then_inc(s_full[n % NS], 1)
                    if half == 1:
                        n = score_no[(b, g, "x", HG)]
                        ps = next_scores(n)
                        for j in range(HG):
                            r = slice(32 * j, 32 * j + 32)
                            ins = pe.matmul(ps[r, :], k2_s[r, g, b, P:CW], q16_s[r, b, g, :], start=True, stop=True)
                        ins.then_inc(s_full[n % NS], 1)
                elif stage == "values2":
                    b, g = arg
                    if group2_no[arg] > 0:
                        pe.wait_ge(o2_moved, group2_no[arg])
                    if g == 0:
                        wait_moved(pe, ("v2a",))
                        wait_moved(pe, ("v2b",))
                    slot = slot2_no[arg]
                    for j in range(HG):
                        n = score_no[(*arg, "x", j)]
                        pe.wait_ge(s_moved[n % NS], n // NS + 1)
                        pe.matmul(obank2[32 * j:32 * j + 32, :], v2a_s[:, b, HG * g + j, :],
                                  prob2_s[:, slot % NP, j, :], start=True, stop=False)
                    n = score_no[(*arg, "x", HG)]
                    pe.wait_ge(s_moved[n % NS], n // NS + 1)
                    for j in range(HG):
                        r = slice(32 * j, 32 * j + NCB)
                        ins = pe.matmul(obank2[32 * j:32 * j + 32, :], v2b_s[r, b, HG * g + j, :],
                                        probb_s[r, slot % 2, :], start=False, stop=True)
                    ins.then_inc(slot2_used, 1)
                elif stage == "joined":
                    b, = arg
                    wait_moved(pe, ("oT", b, G - 1))
                    transposes(("aT", b), lambda t: att_s[:, b, t, :])
                elif stage == "project":
                    b, = arg
                    wait_moved(pe, ("aT", b))
                    ps = take(pe, ("proj", b))
                    for t in range(TT):
                        ins = pe.matmul(ps[:, t * D:(t + 1) * D], xT_s[:, b * L + t * P:b * L + (t + 1) * P], wproj_s[:, :],
                                        start=True, stop=True)
                    ins.then_inc(filled(("proj", b)), 1)
                elif stage == "turn2":
                    b, = arg
                    normed(("x2T", b), b)
                elif stage == "query2":
                    b, = arg
                    wait_moved(pe, ("x2T", b))
                    ps = take(pe, ("q2", b))
                    pe.matmul(ps[:, :], wq_s[:, :], xT_s[:, b * L:(b + 1) * L], start=True,
                              stop=True).then_inc(filled(("q2", b)), 1)
                elif stage == "spread2":
                    b, g = arg
                    r = slice(32 * g, 32 * g + 32)
                    wait_moved(pe, ("q2", b))
                    spread(("sq2", b, g), qhi_s[r, b, :], qlo_s[r, b, :], 0, g)
                elif stage == "turn3":
                    normed(("x3T", arg[0]), arg[0])
                elif stage == "router_hidden":
                    b, m = arg
                    wait_moved(pe, ("x3T", b))
                    pe.wait_ge(in_router, 16 * 3)
                    ps = take(pe, ("r", b, m))
                    pe.matmul(ps[:, :], rw1_s[:, m * P:(m + 1) * P], xT_s[:, b * L:(b + 1) * L], start=True,
                              stop=True).then_inc(filled(("r", b, m)), 1)
                elif stage == "partials":
                    b, = arg
                    for m in range(M):
                        wait_moved(pe, ("r", b, m))
                    ps = take(pe, ("lp", b))
                    for m in range(M):
                        ins = pe.matmul(ps[32 * m:32 * m + 32, :], rw2_s[:, m, :], rT_s[:, m, :], start=True, stop=True)
                    ins.then_inc(filled(("lp", b)), 1)
                elif stage == "logits":
                    b, = arg
                    wait_moved(pe, ("lp", b))
                    ps = take(pe, ("lg", b))
                    for t in range(TT):
                        ins = pe.matmul(ps[:, t * E:(t + 1) * E], partial_s[:, t * P:(t + 1) * P], sum_s, start=True,
                                        stop=True)
                    ins.then_inc(filled(("lg", b)), 1)
                elif stage == "places":
                    b, = arg
                    counts["pick"] += 5
                    pe.wait_ge(pick_done, counts["pick"])
                    ps = take(pe, ("pos", b))
                    for t in range(TT):
                        tile = b * TT + t
                        for s in range(tile + 1):
                            ins = pe.matmul(ps[:, t * E:(t + 1) * E], count_s[:, 0 if s == tile else 1, :],
                                            picks_s[:, s, :], start=(s == 0), stop=(s == tile))
                    ins.then_inc(filled(("pos", b)), 1)
                elif stage == "gates":
                    b, = arg
                    counts["gate"] += 6
                    pe.wait_ge(gate_done, counts["gate"])
                    transposes(("gT", b), lambda t: gate_s[:, b * TT + t, :], rows=E)
                elif stage == "bias_out":
                    b, = arg
                    wait_moved(pe, ("gT", b))
                    ps = take(pe, ("b2", b))
                    for t in range(TT):
                        ins = pe.matmul(ps[:, t * D:(t + 1) * D], gateT_s[:, b, t * P:(t + 1) * P], eb2_s[:, :],
                                        start=True, stop=True)
                    ins.then_inc(filled(("b2", b)), 1)
                elif stage == "hidden":
                    b, e, m = arg
                    if m == 0:
                        pe.wait_ge(weights_done, 2 * e + 2)
                        pe.wait_ge(x3_split, b + 1)
                    ps = take(pe, ("h", b, e, m))
                    c = slice(m * P, (m + 1) * P)
                    pe.matmul(ps[:, :], ew1hi_s[:, e, c], x3hi_s[:, b, :], start=True, stop=False)
                    pe.matmul(ps[:, :], ew1hi_s[:, e, c], x3lo_s[:, b, :], start=False, stop=False)
                    pe.matmul(ps[:, :], ew1lo_s[:, e, c], x3hi_s[:, b, :], start=False,
                              stop=True).then_inc(filled(("h", b, e, m)), 1)
                elif stage == "expert_out":
                    b, e, t = arg
                    i = b * E + e
                    if t == 0:
                        pe.wait_ge(h_split, (i + 1) * M)
                        if b == 0 and e == 0:
                            pe.wait_ge(o_moved, B * G)
                        elif b == 1 and e == 1:
                            pe.wait_ge(o2_moved, B * G)
                        else:
                            pe.wait_ge(y_moved, i if b == 0 or e == 0 else i - 1)
                    ps = y_bank(b, e)
                    r = slice(t * P, (t + 1) * P)
                    for m in range(M):
                        c = slice(m * D, (m + 1) * D)
                        hi, lo = hidden_s[i % 3]
                        pairs = ((hi, ew2hi_s), (hi, ew2lo_s), (lo, ew2hi_s))
                        for n, (h, w) in enumerate(pairs):
                            ins = pe.matmul(ps[:, r], h[:, m, r], w[:, e, c], start=(m == 0 and n == 0),
                                            stop=(m == M - 1 and n == 2))
                    if t == TT - 1:
                        ins.then_inc(y_full, 1)
                elif stage == "heads1":
                    n = group_no[arg]
                    pe.wait_ge(o_moved, n + 1)
                    transposes(("oT", *arg), lambda t: o_s[:, n % 2, t * P:(t + 1) * P])
                elif stage == "heads2":
                    n = group2_no[arg]
                    pe.wait_ge(o2_moved, n + 1)
                    transposes(("oT2", *arg), lambda t: o2_s[:, n % 2, t * P:(t + 1) * P])


def constants():
    pos = (np.arange(L, dtype=np.float32) * np.float32((1.0 + np.sqrt(5.0)) / 2.0)) % np.float32(1.0)
    bias = np.exp(-np.abs(pos[:, None] - pos[None, :])) + np.float32(1e-8)
    spread = np.zeros((P, 4, P), np.float16)
    for kind, parts in enumerate(((0, 1), (2,), (0, 2), (1,))):
        for j in range(HG):
            for t in parts:
                for d in range(DH):
                    spread[j * DH + d::32, kind, 32 * j + t * DH + d] = 1
    count = np.stack([np.triu(np.ones((P, P), np.float16), 1), np.ones((P, P), np.float16)], 1)
    size = np.zeros((P, 32), np.float16)
    shift = np.zeros((P, 1), np.float32)
    for h in range(H):
        size[h * DH:(h + 1) * DH, h] = 1
    for j in range(HG):
        shift[32 * j + 3 * DH:32 * j + 3 * DH + 2] = -SHIFT
    total = np.zeros((P, E), np.float32)
    for m in range(M):
        total[32 * m:32 * m + E] = np.eye(E)
    iota = np.tile(np.arange(E, dtype=np.float32), (P, 1))
    return {
        "bias": np.ascontiguousarray(bias.astype(np.float32).reshape(KC, P, L).transpose(1, 0, 2)),
        "full": np.concatenate([np.eye(P, dtype=np.float32), iota, shift, total], 1),
        "half": np.concatenate([spread.reshape(P, -1), count.reshape(P, -1), size], 1),
    }


def kernel(x, ctx_768, L0_attn_w_qkv, L0_attn_w_proj, L0_attn_b_proj, L0_xattn_norm_g, L0_xattn_norm_b,
           L0_xattn_tnorm_g, L0_xattn_tnorm_b, L0_xattn_Wq, L0_xattn_bq, L0_xattn_Wk, L0_xattn_bk, L0_xattn_Wv,
           L0_xattn_bv, L0_ffn_rw1, L0_ffn_rb1, L0_ffn_rw2, L0_ffn_rb2, L0_ffn_ew1, L0_ffn_eb1, L0_ffn_ew2,
           L0_ffn_eb2):
    import concourse.bacc as _bacc
    from concourse.bass_utils import run_bass_kernel_spmd as _run

    nc = _bacc.Bacc("TRN2", target_bir_lowering=False, num_devices=1)
    fill = np.zeros(P - CD, np.float32)
    vectors = np.concatenate([np.asarray(v) for v in (
        L0_ffn_eb1.reshape(-1), L0_ffn_rb1, L0_xattn_norm_g, L0_xattn_norm_b, L0_xattn_bq, L0_xattn_bk,
        L0_xattn_tnorm_g, fill, L0_xattn_tnorm_b, fill)]).reshape(VROWS, P)
    rows = np.concatenate([np.asarray(v) for v in (L0_attn_b_proj, L0_xattn_bv, L0_ffn_rb2)])
    wkv = np.concatenate([np.asarray(L0_xattn_Wk), np.asarray(L0_xattn_Wv)], 1)
    given = {"x": x, "ctx_in": ctx_768, "w_qkv": L0_attn_w_qkv, "w_proj": L0_attn_w_proj, "wq": L0_xattn_Wq,
             "rw1": L0_ffn_rw1, "rw2": L0_ffn_rw2, "ew1": L0_ffn_ew1, "ew2": L0_ffn_ew2, "eb2": L0_ffn_eb2,
             "wkv": wkv, "vectors": vectors, "rows": rows}
    given.update({f"c_{k}": v for k, v in constants().items()})
    arrays, args = {}, {}
    for name, a in given.items():
        a = np.ascontiguousarray(a)
        arrays[name] = a
        args[name] = nc.dram_tensor(name, a.shape, mybir.dt.from_np(a.dtype), kind="ExternalInput").ap()
    out = nc.dram_tensor("out", (B, L, D), F32, kind="ExternalOutput").ap()
    build(nc, out=out, **args)
    r = _run(nc, [arrays], core_ids=[0])
    return r.results[0]["out"]
```
